# Optimizing a Trainium2 kernel written in Bass

```python
import numpy as np
import jax
import jax.numpy as jnp

def _softmax(x, axis=-1):
    return jax.nn.softmax(x, axis=axis)

def _gelu(x):
    return jax.nn.gelu(x, approximate=True)

def _silu(x):
    return jax.nn.silu(x)

def _sigmoid(x):
    return jax.nn.sigmoid(x)

def _layernorm(x, axis=-1, eps=1e-05):
    m = jnp.mean(x, axis=axis, keepdims=True)
    v = jnp.var(x, axis=axis, keepdims=True)
    return (x - m) / jnp.sqrt(v + eps)

def _scatter_add(tgt, idx, src, axis=0):
    return tgt.at[idx].add(src)

def _segment_sum(src, seg, n):
    return jax.ops.segment_sum(src, seg, n)
kernel_name = 'mk_gnn_preln_d4_gnn_r8_58c040'

def setup_inputs(seed: int=0):
    np.random.seed(seed)
    _w = jnp.asarray

    def _rec_inputs():
        import jax
        import jax.numpy as jnp
        _gk = jax.random.key(seed)
        x = -8.776e-05 + 1 * jax.random.normal(jax.random.fold_in(_gk, 1), (6250, 128), jnp.float32)
        _s = jax.random.randint(jax.random.fold_in(_gk, 2), (50000,), 0, 6250, jnp.int32)
        _d = jax.random.randint(jax.random.fold_in(_gk, 3), (50000,), 0, 6250, jnp.int32)
        _loop = jnp.arange(6250, dtype=jnp.int32)
        src = jnp.concatenate([_s, _d, _loop])
        dst = jnp.concatenate([_d, _s, _loop])
        _o = jnp.argsort(dst, stable=True)
        src = src[_o]
        dst = dst[_o]
        edge_type_2 = jax.random.randint(jax.random.fold_in(_gk, 12), (106250,), 0, 2, jnp.int32)
        return (x, src, dst, edge_type_2)
    x, src, dst, edge_type_2 = _rec_inputs()

    def _L0_gnn_setup():
        import jax, jax.numpy as jnp
        import numpy as np
        N = 5000
        E = 80000
        IN = 128
        H = 4
        C = 32
        key = jax.random.key(seed)
        ks = jax.random.split(key, 5)
        x = jax.random.normal(ks[0], (N, IN), dtype=jnp.float32)
        edge_index = jax.random.randint(ks[1], (2, E), 0, N, dtype=jnp.int64)
        W_lin = jax.random.normal(ks[2], (IN, H * C), dtype=jnp.float32) * 0.05
        b_lin = jnp.zeros((H * C,), dtype=jnp.float32)
        W_att = jax.random.normal(ks[3], (2 * H * C, H), dtype=jnp.float32) * 0.05
        b_att = jnp.zeros((H,), dtype=jnp.float32)
        return {'x': x, 'edge_index': edge_index, 'W_lin': W_lin, 'b_lin': b_lin, 'W_att': W_att, 'b_att': b_att}
    _L0_gnn_all = _L0_gnn_setup()
    _L0_gnn_in = {k: v for k, v in _L0_gnn_all.items() if k in ('W_lin', 'b_lin', 'W_att', 'b_att')}
    del _L0_gnn_all

    def _L1_gnn_setup():
        import jax, jax.numpy as jnp
        import numpy as np
        IN_DIM = 128
        OUT_DIM = 128
        N_NODES = 1250
        N_EDGES = 80000
        key = jax.random.key(seed)
        ks = jax.random.split(key, 9)
        X = jax.random.normal(ks[0], (N_NODES, IN_DIM), dtype=jnp.float32)
        edge_index = jax.random.randint(ks[1], (2, N_EDGES), 0, N_NODES, dtype=jnp.int64)
        edge_types = jax.random.randint(ks[2], (N_EDGES,), 0, 2, dtype=jnp.int64)
        s = 1.0 / np.sqrt(IN_DIM)
        W_data = jax.random.uniform(ks[3], (OUT_DIM, IN_DIM), minval=-s, maxval=s, dtype=jnp.float32)
        b_data = jax.random.uniform(ks[4], (OUT_DIM,), minval=-s, maxval=s, dtype=jnp.float32)
        W_control = jax.random.uniform(ks[5], (OUT_DIM, IN_DIM), minval=-s, maxval=s, dtype=jnp.float32)
        b_control = jax.random.uniform(ks[6], (OUT_DIM,), minval=-s, maxval=s, dtype=jnp.float32)
        W_self = jax.random.uniform(ks[7], (OUT_DIM, IN_DIM), minval=-s, maxval=s, dtype=jnp.float32)
        b_self = jax.random.uniform(ks[8], (OUT_DIM,), minval=-s, maxval=s, dtype=jnp.float32)
        return {'X': X, 'edge_index': edge_index, 'edge_types': edge_types, 'W_data': W_data, 'b_data': b_data, 'W_control': W_control, 'b_control': b_control, 'W_self': W_self, 'b_self': b_self}
    _L1_gnn_all = _L1_gnn_setup()
    _L1_gnn_in = {k: v for k, v in _L1_gnn_all.items() if k in ('W_data', 'b_data', 'W_control', 'b_control', 'W_self', 'b_self')}
    del _L1_gnn_all

    def _L2_gnn_setup():
        import jax, jax.numpy as jnp
        import numpy as np
        N_NODES = 12500

        def _gcn_conv(x, src, dst, W, b, n_nodes):
            h = x @ W
            deg = jax.ops.segment_sum(jnp.ones_like(dst, dtype=h.dtype), dst, num_segments=n_nodes)
            dinv = jnp.where(deg > 0, jax.lax.rsqrt(deg), 0.0)
            norm = dinv[src] * dinv[dst]
            msg = norm[:, None] * h[src]
            out = jax.ops.segment_sum(msg, dst, num_segments=n_nodes)
            return out + b
        key = jax.random.key(seed)
        k1, k2, k3, k4, k5, k6 = jax.random.split(key, 6)
        d_in, d_hid = (128, 128)
        x = jax.random.normal(k1, (N_NODES, d_in), dtype=jnp.float32)
        edge_index = jax.random.randint(k2, (2, 200000), 0, N_NODES, dtype=jnp.int64)
        s1 = 1.0 / np.sqrt(d_in)
        s2 = 1.0 / np.sqrt(d_hid)
        W1 = jax.random.uniform(k3, (d_in, d_hid), jnp.float32, -s1, s1)
        b1 = jnp.zeros((d_hid,), jnp.float32)
        W2 = jax.random.uniform(k4, (d_hid, d_hid), jnp.float32, -s2, s2)
        b2 = jnp.zeros((d_hid,), jnp.float32)
        return {'x': x, 'edge_index': edge_index, 'W1': W1, 'b1': b1, 'W2': W2, 'b2': b2}
    _L2_gnn_all = _L2_gnn_setup()
    _L2_gnn_in = {k: v for k, v in _L2_gnn_all.items() if k in ('W1', 'b1', 'W2', 'b2')}
    del _L2_gnn_all

    def _L3_gnn_setup():
        import jax, jax.numpy as jnp
        import numpy as np
        N_NODES = 12500
        N_EDGES = 200000
        D_IN = 128
        D_HID = 32
        key = jax.random.key(seed)
        k1, k2, k3, k4, k5 = jax.random.split(key, 5)
        x = jax.random.normal(k1, (N_NODES, D_IN), dtype=jnp.float32)
        edge_index = jax.random.randint(k2, (2, N_EDGES), 0, N_NODES, dtype=jnp.int64)
        W1 = jax.random.normal(k3, (D_IN, D_HID), dtype=jnp.float32) / np.sqrt(D_IN)
        b1 = jnp.zeros((D_HID,), dtype=jnp.float32)
        W2 = jax.random.normal(k4, (D_HID, D_IN), dtype=jnp.float32) / np.sqrt(D_HID)
        b2 = jnp.zeros((D_IN,), dtype=jnp.float32)
        return {'x': x, 'edge_index': edge_index, 'W1': W1, 'b1': b1, 'W2': W2, 'b2': b2}
    _L3_gnn_all = _L3_gnn_setup()
    _L3_gnn_in = {k: v for k, v in _L3_gnn_all.items() if k in ('W1', 'b1', 'W2', 'b2')}
    del _L3_gnn_all
    return {'x': x, 'src': src, 'dst': dst, 'edge_type_2': edge_type_2, 'L0_gnn_W_lin': _L0_gnn_in['W_lin'], 'L0_gnn_b_lin': _L0_gnn_in['b_lin'], 'L0_gnn_W_att': _L0_gnn_in['W_att'], 'L0_gnn_b_att': _L0_gnn_in['b_att'], 'L1_gnn_W_data': _L1_gnn_in['W_data'], 'L1_gnn_b_data': _L1_gnn_in['b_data'], 'L1_gnn_W_control': _L1_gnn_in['W_control'], 'L1_gnn_b_control': _L1_gnn_in['b_control'], 'L1_gnn_W_self': _L1_gnn_in['W_self'], 'L1_gnn_b_self': _L1_gnn_in['b_self'], 'L2_gnn_W1': _L2_gnn_in['W1'], 'L2_gnn_b1': _L2_gnn_in['b1'], 'L2_gnn_W2': _L2_gnn_in['W2'], 'L2_gnn_b2': _L2_gnn_in['b2'], 'L3_gnn_W1': _L3_gnn_in['W1'], 'L3_gnn_b1': _L3_gnn_in['b1'], 'L3_gnn_W2': _L3_gnn_in['W2'], 'L3_gnn_b2': _L3_gnn_in['b2']}

def reference(x, src, dst, edge_type_2, L0_gnn_W_lin, L0_gnn_b_lin, L0_gnn_W_att, L0_gnn_b_att, L1_gnn_W_data, L1_gnn_b_data, L1_gnn_W_control, L1_gnn_b_control, L1_gnn_W_self, L1_gnn_b_self, L2_gnn_W1, L2_gnn_b1, L2_gnn_W2, L2_gnn_b2, L3_gnn_W1, L3_gnn_b1, L3_gnn_W2, L3_gnn_b2):
    import jax
    import jax.numpy as jnp

    def _L0_gnn_ref(x, edge_index, W_lin, b_lin, W_att, b_att):
        import jax, jax.numpy as jnp
        import numpy as np
        N = 5000
        E = 80000
        IN = 128
        H = 4
        C = 32
        n = x.shape[0]
        row, col = (edge_index[0], edge_index[1])
        xl = x @ W_lin + b_lin
        hc = xl.shape[1]
        s_i = xl @ W_att[:hc]
        s_j = xl @ W_att[hc:]
        alpha = s_i[row] + s_j[col] + b_att
        alpha = jnp.where(alpha >= 0, alpha, 0.2 * alpha)
        amax = jax.ops.segment_max(alpha, row, num_segments=n)
        alpha = jnp.exp(alpha - amax[row])
        asum = jax.ops.segment_sum(alpha, row, num_segments=n)
        alpha = alpha / (asum[row] + 1e-16)
        xh = xl.reshape(n, H, C)
        msg = alpha[:, :, None] * xh[row]
        out = jax.ops.segment_sum(msg, col, num_segments=n)
        deg = jax.ops.segment_sum(jnp.ones((row.shape[0],), xl.dtype), col, num_segments=n)
        out = jnp.where(deg[:, None, None] > 0, out, xh)
        return out.reshape(n, H * C)

    def _L1_gnn_ref(X, edge_index, edge_types, W_data, b_data, W_control, b_control, W_self, b_self):
        import jax, jax.numpy as jnp
        import numpy as np
        IN_DIM = 128
        OUT_DIM = 128
        N_NODES = 1250
        N_EDGES = 80000
        src, dst = (edge_index[0], edge_index[1])
        Xs = X[src]
        m_data = Xs @ W_data.T + b_data
        m_ctrl = Xs @ W_control.T + b_control
        msg = jnp.where((edge_types == 0)[:, None], m_data, m_ctrl)
        agg = jax.ops.segment_sum(msg, dst, num_segments=X.shape[0])
        out = agg + (X @ W_self.T + b_self)
        return jax.nn.relu(out)

    def _L2_gnn_ref(x, edge_index, W1, b1, W2, b2):
        import jax, jax.numpy as jnp
        import numpy as np
        N_NODES = 12500

        def _gcn_conv(x, src, dst, W, b, n_nodes):
            h = x @ W
            deg = jax.ops.segment_sum(jnp.ones_like(dst, dtype=h.dtype), dst, num_segments=n_nodes)
            dinv = jnp.where(deg > 0, jax.lax.rsqrt(deg), 0.0)
            norm = dinv[src] * dinv[dst]
            msg = norm[:, None] * h[src]
            out = jax.ops.segment_sum(msg, dst, num_segments=n_nodes)
            return out + b
        n = x.shape[0]
        loop = jnp.arange(n, dtype=edge_index.dtype)
        src = jnp.concatenate([edge_index[0], loop])
        dst = jnp.concatenate([edge_index[1], loop])
        h = jax.nn.relu(_gcn_conv(x, src, dst, W1, b1, n))
        h = jax.nn.relu(_gcn_conv(h, src, dst, W2, b2, n))
        return h

    def _L3_gnn_ref(x, edge_index, W1, b1, W2, b2):
        import jax, jax.numpy as jnp
        import numpy as np
        N_NODES = 12500
        N_EDGES = 200000
        D_IN = 128
        D_HID = 32
        N = x.shape[0]
        loop = jnp.arange(N, dtype=edge_index.dtype)
        src = jnp.concatenate([edge_index[0], loop])
        dst = jnp.concatenate([edge_index[1], loop])
        deg = jax.ops.segment_sum(jnp.ones_like(dst, dtype=jnp.float32), dst, num_segments=N)
        dinv = jax.lax.rsqrt(deg)
        norm = dinv[src] * dinv[dst]

        def gcn_conv(h, W, b):
            h = h @ W
            msg = h[src] * norm[:, None]
            out = jax.ops.segment_sum(msg, dst, num_segments=N)
            return out + b
        h = gcn_conv(x.astype(jnp.float32), W1, b1)
        h = gcn_conv(h, W2, b2)
        return jax.nn.relu(h)
    edge_index = jnp.stack([src, dst])
    h = jnp.maximum(_layernorm(x, axis=-1), 0.0)
    x = x + _L0_gnn_ref(h, edge_index, L0_gnn_W_lin, L0_gnn_b_lin, L0_gnn_W_att, L0_gnn_b_att)
    h = jnp.maximum(_layernorm(x, axis=-1), 0.0)
    x = x + _L1_gnn_ref(h, edge_index, edge_type_2, L1_gnn_W_data, L1_gnn_b_data, L1_gnn_W_control, L1_gnn_b_control, L1_gnn_W_self, L1_gnn_b_self)
    h = jnp.maximum(_layernorm(x, axis=-1), 0.0)
    x = x + _L2_gnn_ref(h, edge_index, L2_gnn_W1, L2_gnn_b1, L2_gnn_W2, L2_gnn_b2)
    h = jnp.maximum(_layernorm(x, axis=-1), 0.0)
    x = x + _L3_gnn_ref(h, edge_index, L3_gnn_W1, L3_gnn_b1, L3_gnn_W2, L3_gnn_b2)
    return x

_drawn_inputs = setup_inputs


def setup_inputs(seed=0):
    import zlib

    import numpy as np

    out = dict(_drawn_inputs(seed))
    spreads = {'L0_gnn_b_lin': (0.0, 0.1),
     'L0_gnn_b_att': (0.0, 0.8),
     'L2_gnn_b1': (0.0, 0.8),
     'L2_gnn_b2': (0.0, 0.335),
     'L3_gnn_b1': (0.0, 0.1),
     'L3_gnn_b2': (0.0, 0.311)}
    factors = {'L0_gnn_W_att': 3.142, 'L1_gnn_b_self': 3.878}
    for name, (base, spread) in spreads.items():
        noise = np.random.default_rng([zlib.crc32(name.encode()), seed]).standard_normal(out[name].shape)
        drawn = base * np.exp(spread * noise) if base else spread * noise
        out[name] = jnp.asarray(drawn.astype(out[name].dtype))
    for name, factor in factors.items():
        out[name] = (out[name] * factor).astype(out[name].dtype)
    return out
```

```python
import concourse.bass as bass
from concourse import mybir
from contextlib import ExitStack, contextmanager

fp32 = mybir.dt.float32
bf16 = mybir.dt.bfloat16
i32 = mybir.dt.int32
ALU = mybir.AluOpType
ACT = mybir.ActivationFunctionType
AX = mybir.AxisListType

P = 128
N = 6250
E = 106250
D = 128
NH, HC = 4, 32
D3 = 32
NT = (N + P - 1) // P
NP = NT * P
U = 8
G2 = 2 * U
STEPS = -(-(E + N) // (P * G2))
J = STEPS * G2
EP = J * P
LAST = NP - 1
AW = D + 2 * NH
BIG = 1e30
NG = 7
LN_EPS = 1e-5


def bc(ap, shape):
    return ap.to_broadcast(shape)


@contextmanager
def semaphores(nc, *names):
    sems = [nc.alloc_semaphore(f"{name}_{nc.next_id()}") for name in names]
    yield sems
    nc.clear_and_free_semaphores(sems)
    nc.all_engine_barrier()


def pass_gate(nc, gate):
    return nc.gpsimd.tensor_tensor(gate[:, 2:3], gate[:, 0:1], gate[:, 1:2], ALU.add)


class Count:

    def __init__(self, sem):
        self.sem, self.n = sem, 0

    def link(self, engine, ins):
        self.n += 1
        ins.then_inc(self.sem, 1)
        engine.wait_ge(self.sem, self.n)


def gnn_kernel(nc, x, e_src, e_dst, e_type, W0, b0, Watt, batt, Wd, bd, Wc, bcn, Ws, bs,
               W21, b21, W22, b22, W31, b31, W32, b32, out):
    ctx = ExitStack()

    credit = nc.dram_tensor("credit", (2, 2), fp32).ap()
    edges = nc.dram_tensor("edges_by_dst", (EP, 4), fp32).ap()
    sj_node = nc.dram_tensor("sj_node", (NP, NH), fp32).ap()
    sj_start = nc.dram_tensor("sj_start", (EP + NP, NH), fp32).ap()
    sj_edge = nc.dram_tensor("sj_edge", (EP, NH), fp32).ap()
    by_src = nc.dram_tensor("by_src", (EP, 2 * NH), fp32).ap()
    max_scan = nc.dram_tensor("max_scan", (EP, NH), fp32).ap()
    sum_scan = nc.dram_tensor("sum_scan", (EP, NH), fp32).ap()
    row_node = nc.dram_tensor("row_node", (NP, 2 * NH), fp32).ap()
    row_start = nc.dram_tensor("row_start", (EP + NP, 2 * NH), fp32).ap()
    table0 = nc.dram_tensor("table0", (NP, AW), fp32).ap()
    table1 = nc.dram_tensor("table1", (3 * NP, D), fp32).ap()
    table2 = [nc.dram_tensor(f"table2{c}", (NP, D), fp32).ap() for c in "ab"]
    table3 = [nc.dram_tensor(f"table3{c}", (NP, D3), fp32).ap() for c in "ab"]

    with ctx:
        def sb(name, shape, dt=fp32, c=ctx):
            return c.enter_context(nc.sbuf_tensor(name, shape, dt))

        X = sb("X", [P, NT, D])
        H = sb("H", [P, NT, D])
        acc = sb("acc", [P, NP + P])
        ident = sb("ident", [P, P])
        iota_row = sb("iota_row", [P, P])
        iota_col = sb("iota_col", [P, 1])
        ones = sb("ones", [P, P])
        above = sb("above", [P, P])
        zero_w = sb("zero_w", [P, P], bf16)
        gate = sb("gate", [1, 3])
        count = sb("count", [P, 2, NT])
        offset = sb("offset", [P, 2, NT])
        idx = sb("idx", [P, J], i32)
        idx_typed = sb("idx_typed", [P, J], i32)
        dloc = sb("dloc", [P, J])
        d0i = sb("d0i", [1, J], i32)
        real = sb("real", [P, J])
        dinv = sb("dinv", [P, NT])
        alone = sb("alone", [P, NT])
        w = {"0": sb("w0", [P, D]), "att": sb("watt", [P, 2 * NH]), "1": sb("w1", [P, 3, D]), "21": sb("w21", [P, D]),
             "22": sb("w22", [P, D]), "31": sb("w31", [P, D3]), "32": sb("w32", [D3, D])}
        brow = sb("brow", [1, 4, D])
        batt_row = sb("batt_row", [1, 2 * NH])
        ball = sb("ball", [P, 3, D])
        b31_all = sb("b31_all", [P, D3])

        sort_edges(nc, locals())
        edge_lists(nc, locals())
        load_all(nc, locals())
        layers(nc, locals())
    return


def sort_edges(nc, k):
    ident, iota_row, iota_col, ones, above = (k[n] for n in ("ident", "iota_row", "iota_col", "ones", "above"))
    count, offset, edges = k["count"], k["offset"], k["edges"]
    with ExitStack() as c:
        def sb(name, shape, dt=fp32):
            return c.enter_context(nc.sbuf_tensor(name, shape, dt))

        raw = sb("raw", [P, 3, J], i32)
        key = sb("key", [P, 2, J], i32)
        part = sb("part", [P, 2, J], i32)
        klo = sb("klo", [P, 2, J], bf16)
        khi = sb("khi", [P, 2, J], bf16)
        iota_i = sb("iota_i", [P, P + 1], i32)
        iota_b = sb("iota_b", [P, P], bf16)
        ident_b = sb("ident_b", [P, P], bf16)
        above_b = sb("above_b", [P, P], bf16)
        zeros = sb("zeros", [P, P], bf16)

        with ExitStack() as s:
            loaded, iota_ready, steps = s.enter_context(semaphores(nc, "loaded", "iota_ready", "steps"))
            block = s.enter_context(nc.Block())

            @block.sync
            def _(sp):
                for n, a in enumerate((k["e_src"], k["e_dst"], k["e_type"])):
                    sp.dma_start(raw[:, n, :], a).then_inc(loaded, 16)
                sp.wait_ge(loaded, 48)

            @block.gpsimd
            def _(pool):
                nc.gpsimd.iota(iota_i[:, 0:P], [[1, P]], base=0, channel_multiplier=0).then_inc(iota_ready, 1)
                nc.gpsimd.iota(iota_i[:, P:P + 1], [[1, 1]], base=0, channel_multiplier=1).then_inc(iota_ready, 1)

            @block.vector
            def _(dve):
                v, ch = nc.vector, Count(steps)
                v.memset(ones[:], 1.0)
                v.memset(zeros[:], 0.0)
                v.memset(k["zero_w"][:], 0.0)
                v.memset(k["gate"][:], 0.0)
                dve.wait_ge(iota_ready, 2)
                v.tensor_copy(iota_row[:], iota_i[:, 0:P])
                ch.link(dve, v.tensor_copy(iota_col[:], iota_i[:, P:P + 1]))
                v.tensor_copy(iota_b[:], iota_row[:])
                v.tensor_scalar(ident[:], iota_row[:], iota_col[:, 0:1], None, ALU.is_equal)
                v.tensor_scalar(above[:], iota_row[:], iota_col[:, 0:1], None, ALU.is_gt)
                v.tensor_scalar(ident_b[:], iota_row[:], iota_col[:, 0:1], None, ALU.is_equal)
                v.tensor_scalar(above_b[:], iota_row[:], iota_col[:, 0:1], None, ALU.is_gt)
                dve.wait_ge(loaded, 48)
                v.tensor_copy(key[:, 0, :], raw[:, 1, :])
                ch.link(dve, v.tensor_scalar(key[:, 1, :], raw[:, 2, :], 2.0, float(LAST), ALU.is_equal, ALU.mult))
                ch.link(dve, v.tensor_tensor(key[:, 1, :], key[:, 1, :], raw[:, 0, :], ALU.max))
                ch.link(dve, v.tensor_scalar(part[:], key[:], P - 1, None, ALU.bitwise_and))
                ch.link(dve, v.tensor_copy(klo[:], part[:]))
                ch.link(dve, v.tensor_scalar(part[:], key[:], 7, None, ALU.logical_shift_right))
                ch.link(dve, v.tensor_copy(khi[:], part[:]))

        def one_hots(dve, lo, hi, keys, j0):
            n = len(keys)
            a, b = keys[0], keys[-1] + 1
            nc.vector.tensor_tensor(
                lo, iota_b[:].unsqueeze(1).unsqueeze(1).to_broadcast([P, n, U, P]),
                klo[:, a:b, bass.ds(j0, U)].unsqueeze(3).to_broadcast([P, n, U, P]), ALU.is_equal)
            return nc.vector.tensor_tensor(
                hi, iota_b[:, 0:NT].unsqueeze(1).unsqueeze(1).to_broadcast([P, n, U, NT]),
                khi[:, a:b, bass.ds(j0, U)].unsqueeze(3).to_broadcast([P, n, U, NT]), ALU.is_equal)

        with ExitStack() as s:
            lo = s.enter_context(nc.sbuf_tensor("lo", [P, 2, 2, U, P], bf16))
            hi = s.enter_context(nc.sbuf_tensor("hi", [P, 2, 2, U, NT], bf16))
            hist = [s.enter_context(nc.psum_tensor(f"hist{n}", [P, 512], fp32)) for n in range(2)]
            prefix = s.enter_context(nc.psum_tensor("prefix", [P, 2, 2, NT], fp32))
            zero_row = s.enter_context(nc.sbuf_tensor("zero_row", [P, NT], fp32))
            incl = s.enter_context(nc.sbuf_tensor("incl", [P, 2, NT], fp32))
            built, used, counted, copied, summed, steps = s.enter_context(semaphores(nc, "built", "used", "counted", "copied", "summed", "steps"))
            block = s.enter_context(nc.Block())

            @block.vector
            def _(dve):
                v, ch = nc.vector, Count(steps)
                v.memset(zero_row[:], 0.0)
                with dve.Fori(0, STEPS) as i:
                    for g in range(2):
                        dve.wait_ge(used, i * 2 + (g + 1))
                        one_hots(dve, lo[:, g], hi[:, g], (0, 1), i * G2 + g * U).then_inc(built, 1)
                dve.wait_ge(counted, 1)
                for n in range(2):
                    last = v.tensor_copy(count[:, n, :], hist[n][:, 0:NT])
                last.then_inc(copied, 1)
                dve.wait_ge(summed, 1)
                for n in range(2):
                    ch.link(dve, v.tensor_tensor_scan(incl[:, n, :], prefix[:, 1, n, :], zero_row[:], 0.0, ALU.add, ALU.add))
                ch.link(dve, v.tensor_tensor(incl[:], incl[:], prefix[:, 1], ALU.subtract))
                ch.link(dve, v.tensor_tensor(offset[:], incl[:], prefix[:, 0], ALU.add))

            @block.tensor
            def _(pe):
                for n in range(2):
                    last = nc.tensor.matmul(hist[n][:, 0:NT], zeros[:], zeros[:, 0:NT], start=True, stop=False)
                last.then_inc(used, 2)
                with pe.Fori(0, STEPS) as i:
                    for g in range(2):
                        pe.wait_ge(built, i * 2 + (g + 1))
                        for n in range(2):
                            for u in range(U):
                                last = nc.tensor.matmul(hist[n][:, 0:NT], lo[:, g, n, u, :], hi[:, g, n, u, :],
                                                        start=False, stop=False)
                        last.then_inc(used, 1)
                for n in range(2):
                    last = nc.tensor.matmul(hist[n][:, 0:NT], zeros[:], zeros[:, 0:NT], start=False, stop=True)
                last.then_inc(counted, 1)
                pe.wait_ge(copied, 1)
                for n in range(2):
                    nc.tensor.matmul(prefix[:, 0, n, :], above[:], count[:, n, :], start=True, stop=True)
                    last = nc.tensor.matmul(prefix[:, 1, n, :], ones[:], count[:, n, :], start=True, stop=True)
                last.then_inc(summed, 1)

        with ExitStack() as s:
            def tb(name, shape, dt=fp32):
                return s.enter_context(nc.sbuf_tensor("place_" + name, shape, dt))

            lo = tb("lo", [P, 2, U, P], bf16)
            hi = tb("hi", [P, 2, U, NT], bf16)
            loT = tb("loT", [P, 2, U, P])
            same = tb("same", [P, 2, U, P], bf16)
            base = tb("base", [P, 2, U + 1, NT])
            stage = tb("stage", [P, 2, U], bf16)
            picked = tb("picked", [P, 2, U, NT])
            place = tb("place", [P, U])
            place_i = tb("place_i", [P, 2, U], i32)
            row = tb("row", [P, 2, U, 4])
            lorow = [s.enter_context(nc.psum_tensor(f"lorow{n}", [P, U, P], bf16)) for n in range(2)]
            cum = [s.enter_context(nc.psum_tensor(f"cum{n}", [P, U + 1, 56], fp32)) for n in range(2)]
            look = [s.enter_context(nc.psum_tensor(f"look{n}", [P, U, NT], fp32)) for n in range(2)]
            names = ("staged", "rows", "spread", "hot", "masks", "cummed", "based", "looked", "muls", "placed", "poss", "plc",
                     "scat0", "scat1", "passed")
            (staged, rows, spread, hot, masks, cummed, based, looked, muls, placed, poss, plc, scat0, scat1, passed) = s.enter_context(semaphores(nc, *names))
            scattered = (scat0, scat1)
            block = s.enter_context(nc.Block())

            @block.scalar
            def _(act):
                with act.Fori(0, STEPS) as i:
                    for g in range(2):
                        j0 = i * G2 + g * U
                        act.wait_ge(spread, i * 4 + (2 * g + 1))
                        nc.scalar.activation(stage[:], klo[:, :, bass.ds(j0, U)], ACT.Copy).then_inc(staged, 1)
                        act.wait_ge(scattered[g], i * (16 * U) + 16)
                        nc.scalar.activation(row[:, g, :, 0:3], raw[:, :, bass.ds(j0, U)].rearrange("p f u -> p u f"),
                                             ACT.Copy).then_inc(rows, 1)

            @block.tensor
            def _(pe):
                pe.sem_inc(spread, 1)
                pe.sem_inc(looked, 1)
                with pe.Fori(0, STEPS) as i:
                    for g in range(2):
                        t = i * 2 + g
                        pe.wait_ge(staged, t + 1)
                        for n in range(2):
                            pe.wait_ge(masks, i * 4 + (2 * g + n + 1))
                            for u in range(U):
                                last = nc.tensor.transpose(lorow[n][:, u, :], stage[:, n, u:u + 1].to_broadcast([P, P]), ident_b[:])
                            last.then_inc(spread, 1)
                        for n in range(2):
                            pe.wait_ge(hot, i * 4 + (2 * g + n + 1))
                            pe.wait_ge(based, i * 4 + (2 * g + n + 1))
                            for u in range(1, U + 1):
                                for w in range(u):
                                    last = nc.tensor.matmul(cum[n][:, u, 0:NT], lo[:, n, w, :], hi[:, n, w, :],
                                                            start=w == 0, stop=w == u - 1)
                            last.then_inc(cummed, 1)
                        for n in range(2):
                            pe.wait_ge(based, i * 4 + (2 * g + n + 3))
                            for u in range(U):
                                nc.tensor.matmul(look[n][:, u, :], loT[:, n, u, :], base[:, n, u, :], start=True, stop=False)
                                last = nc.tensor.matmul(look[n][:, u, :], same[:, n, u, :], hi[:, n, u, :], start=False, stop=True)
                            last.then_inc(looked, 1)

            @block.vector
            def _(dve):
                v = nc.vector
                v.tensor_copy(base[:, :, U, :], offset[:]).then_inc(based, 2)
                dve.sem_inc(masks, 2)
                with dve.Fori(0, STEPS) as i:
                    for g in range(2):
                        j0 = i * G2 + g * U
                        for n in range(2):
                            m = i * 4 + (2 * g + n)
                            dve.wait_ge(spread, m + 2)
                            dve.wait_ge(looked, i * 4 + (2 * g + 1))
                            v.tensor_scalar(loT[:, n], lorow[n][:], iota_col[:, 0:1], None, ALU.is_equal)
                            v.tensor_tensor(same[:, n], lorow[n][:],
                                            klo[:, n, bass.ds(j0, U)].unsqueeze(2).to_broadcast([P, U, P]),
                                            ALU.is_equal).then_inc(masks, 1)
                            one_hots(dve, lo[:, n:n + 1], hi[:, n:n + 1], (n,), j0).then_inc(hot, 1)
                            dve.wait_ge(masks, m + 3)
                            v.tensor_tensor(same[:, n], same[:, n], above_b[:].unsqueeze(1).to_broadcast([P, U, P]), ALU.mult)
                        for n in range(2):
                            m = i * 4 + (2 * g + n)
                            dve.wait_ge(based, m + 2)
                            v.tensor_copy(base[:, n, 0, :], base[:, n, U, :]).then_inc(plc, 1)
                            dve.wait_ge(plc, i * 10 + (5 * g + n + 1))
                            dve.wait_ge(cummed, m + 1)
                            v.tensor_tensor(base[:, n, 1:U + 1, :], cum[n][:, 1:U + 1, 0:NT],
                                            base[:, n, 0:1, :].to_broadcast([P, U, NT]), ALU.add).then_inc(based, 1)
                        for n in range(2):
                            m = i * 4 + (2 * g + n)
                            dve.wait_ge(looked, m + 2)
                            v.tensor_tensor(picked[:, n], look[n][:], hi[:, n], ALU.mult).then_inc(muls, 1)
                            dve.wait_ge(muls, m + 1)
                            if n == 0:
                                v.tensor_reduce(place[:], picked[:, n], AX.X, ALU.add).then_inc(plc, 1)
                            else:
                                dve.wait_ge(rows, i * 2 + (g + 1))
                                v.tensor_reduce(row[:, g, :, 3], picked[:, n], AX.X, ALU.add).then_inc(plc, 1)
                        dve.wait_ge(plc, i * 10 + (5 * g + 4))
                        dve.wait_ge(scattered[g], i * (16 * U) + 16)
                        v.tensor_copy(place_i[:, g], place[:]).then_inc(plc, 1)
                        dve.wait_ge(plc, i * 10 + (5 * g + 5))
                        v.memset(place[:, 0:1], 0.0).then_inc(placed, 1)

            @block.gpsimd
            def _(pool):
                pool.sem_inc(passed, 1)
                for g in range(2):
                    pool.dma_start(k["credit"][g:g + 1, :], k["gate"][:, 0:2]).then_inc(scattered[g], 16)
                with pool.Fori(0, STEPS) as i:
                    for g in range(2):
                        pool.wait_ge(placed, i * 2 + (g + 1))
                        pool.wait_ge(passed, i * 2 + (g + 1))
                        pass_gate(nc, k["gate"]).then_inc(passed, 1)
                        for u in range(U):
                            nc.gpsimd.indirect_dma_start(
                                edges, bass.IndirectOffsetOnAxis(ap=place_i[:, g, u:u + 1], axis=0),
                                row[:, g, u, :], None).then_inc(scattered[g], 16)
                for g in range(2):
                    pool.wait_ge(scattered[g], STEPS * 16 * U + 16)


def edge_lists(nc, k):
    idx, idx_typed, dloc, d0i, real = (k[n] for n in ("idx", "idx_typed", "dloc", "d0i", "real"))
    with ExitStack() as s:
        es = s.enter_context(nc.sbuf_tensor("sorted_chunks", [P, J, 4], fp32))
        d0 = s.enter_context(nc.sbuf_tensor("first_dst", [1, J], fp32))
        root = s.enter_context(nc.sbuf_tensor("root", [P, NT], fp32))
        first = s.enter_context(nc.psum_tensor("first_all", [P, 2, 512], fp32))
        loaded, firsts, spread, rooted, rooting, steps = s.enter_context(semaphores(nc, "loaded", "firsts", "spread", "rooted", "rooting", "steps"))
        block = s.enter_context(nc.Block())
        half = J // 2

        @block.sync
        def _(sp):
            sp.dma_start(es[:], k["edges"].rearrange("(j p) f -> p j f", p=P)).then_inc(loaded, 16)

        @block.vector
        def _(dve):
            v, ch = nc.vector, Count(steps)
            ch.link(dve, v.tensor_scalar(root[:], k["count"][:, 0, :], 1.0, None, ALU.max))
            v.tensor_scalar(k["alone"][:], root[:], 1.0, None, ALU.is_equal).then_inc(rooting, 1)
            dve.wait_ge(loaded, 16)
            v.tensor_copy(d0i[:], es[0:1, :, 1])
            v.tensor_copy(d0[:], es[0:1, :, 1]).then_inc(firsts, 1)
            v.tensor_copy(idx[:], es[:, :, 0])
            v.tensor_scalar(real[:], es[:, :, 2], 2.0, None, ALU.is_lt)
            v.scalar_tensor_tensor(idx_typed[:], es[:, :, 2], float(NP), es[:, :, 0], ALU.mult, ALU.add)
            dve.wait_ge(spread, 1)
            for n in range(2):
                a = slice(n * half, (n + 1) * half)
                v.tensor_tensor(dloc[:, a], es[:, a, 1], first[:, n, 0:half], ALU.subtract)
            dve.wait_ge(rooted, 1)
            v.reciprocal(k["dinv"][:], root[:])

        @block.scalar
        def _(act):
            act.wait_ge(rooting, 1)
            nc.scalar.activation(root[:], root[:], ACT.Sqrt).then_inc(rooted, 1)

        @block.tensor
        def _(pe):
            pe.wait_ge(firsts, 1)
            for n in range(2):
                last = nc.tensor.matmul(first[:, n, 0:half], k["ones"][0:1, :], d0[0:1, n * half:(n + 1) * half],
                                        start=True, stop=True)
            last.then_inc(spread, 1)


def layer_norm(nc, k, tag):
    X, H = k["X"], k["H"]
    with ExitStack() as s:
        stat = s.enter_context(nc.sbuf_tensor(tag + "_stat", [P, NT], fp32))
        rstd = s.enter_context(nc.sbuf_tensor(tag + "_rstd", [P, NT], fp32))
        square = k["acc"][:, 0:NP].rearrange("p (t d) -> p t d", d=D)
        steps, squared, spread, rooted = s.enter_context(semaphores(nc, "steps", "squared", "spread", "rooted"))
        block = s.enter_context(nc.Block())
        wide = lambda t: t[:].unsqueeze(2).to_broadcast([P, NT, D])

        @block.vector
        def _(dve):
            v, ch = nc.vector, Count(steps)
            ch.link(dve, v.tensor_reduce(stat[:], X[:], AX.X, ALU.add))
            ch.link(dve, v.tensor_scalar(stat[:], stat[:], 1.0 / D, None, ALU.mult))
            v.tensor_tensor(H[:], X[:], wide(stat), ALU.subtract).then_inc(spread, 1)
            dve.wait_ge(squared, 1)
            ch.link(dve, v.tensor_reduce(stat[:], square, AX.X, ALU.add))
            v.tensor_scalar(stat[:], stat[:], 1.0 / D, LN_EPS, ALU.mult, ALU.add).then_inc(spread, 1)
            dve.wait_ge(rooted, 1)
            ch.link(dve, v.reciprocal(rstd[:], stat[:]))
            ch.link(dve, v.tensor_tensor(H[:], H[:], wide(rstd), ALU.mult))
            v.tensor_scalar(H[:], H[:], 0.0, None, ALU.max)

        @block.scalar
        def _(act):
            act.wait_ge(spread, 1)
            nc.scalar.activation(square, H[:], ACT.Square).then_inc(squared, 1)
            act.wait_ge(spread, 2)
            nc.scalar.activation(stat[:], stat[:], ACT.Sqrt).then_inc(rooted, 1)


def node_loop(nc, k, tag, source, dest, weight=None, bias=None, turn=True, feat=D, width=D, take=None):
    ident, ones = k["ident"], k["ones"]
    flat = len(source.shape) == 2
    with ExitStack() as s:
        turned = s.enter_context(nc.sbuf_tensor(tag + "_turned", [P, NG, P], fp32))
        pt = s.enter_context(nc.psum_tensor(tag + "_pt", [P, NG + 1, P], fp32))
        pm = s.enter_context(nc.psum_tensor(tag + "_pm", [P, NG + 1, P], fp32))
        tiles = s.enter_context(nc.sbuf_tensor(tag + "_tiles", [P, NG, P], fp32))
        staged, flipped, kept, made, taken = s.enter_context(
            semaphores(nc, "staged", "flipped", "kept", "made", "taken"))
        block = s.enter_context(nc.Block())
        rows_in = feat if flat else P
        read = flipped if turn else made

        @block.scalar
        def _(act):
            act.sem_inc(kept, 1)
            with act.Fori(0, NT // NG) as i:
                act.wait_ge(read, i + 1)
                of = source[0:feat, bass.ds(i * (NG * P), NG * P)] if flat else \
                    source[:, bass.ds(i * NG, NG), :].rearrange("p t d -> p (t d)")
                nc.scalar.activation(tiles[0:rows_in].rearrange("p t d -> p (t d)"), of, ACT.Copy).then_inc(staged, 1)
                if turn and weight is not None:
                    act.wait_ge(flipped, i + 2)
                    act.wait_ge(made, i + 1)
                    nc.scalar.activation(turned[:], pt[:, 0:NG, :], ACT.Copy).then_inc(kept, 1)

        @block.tensor
        def _(pe):
            pe.sem_inc(flipped, 1)
            pe.sem_inc(made, 1)
            with pe.Fori(0, NT // NG) as i:
                pe.wait_ge(staged, i + 1)
                if turn:
                    pe.wait_ge(kept if weight is not None else taken, i + 1)
                    for u in range(NG):
                        last = nc.tensor.transpose(pt[:, u, 0:rows_in], tiles[0:rows_in, u, :], ident[0:rows_in, 0:rows_in])
                    last.then_inc(flipped, 1)
                if weight is not None:
                    if turn:
                        pe.wait_ge(kept, i + 2)
                    pe.wait_ge(taken, i + 1)
                    for u in range(NG):
                        lhs = turned[:, u, :] if turn else tiles[0:rows_in, u, :]
                        last = nc.tensor.matmul(pm[:, u, 0:width], lhs, weight, start=True, stop=bias is None)
                        if bias is not None:
                            last = nc.tensor.matmul(pm[:, u, 0:width], ones[0:1, :], bias, start=False, stop=True)
                    last.then_inc(made, 1)

        @block.vector
        def _(dve):
            dve.sem_inc(taken, 1)
            with dve.Fori(0, NT // NG) as i:
                dve.wait_ge(made if weight is not None else flipped, i + 2)
                got = (pm if weight is not None else pt)[:, 0:NG, 0:width]
                to = dest[:, bass.ds(i * NG, NG), 0:width]
                if take is None:
                    nc.vector.tensor_copy(to, got).then_inc(taken, 1)
                else:
                    take(to, got).then_inc(taken, 1)


def on_vector(nc, tag, *ops):
    with ExitStack() as s:
        [steps] = s.enter_context(semaphores(nc, "steps"))
        block = s.enter_context(nc.Block())

        @block.vector
        def _(dve):
            ch = Count(steps)
            for op in ops:
                ch.link(dve, op(nc.vector))


def store(nc, *pairs):
    with ExitStack() as s:
        [stored] = s.enter_context(semaphores(nc, "stored"))
        block = s.enter_context(nc.Block())

        @block.sync
        def _(sp):
            for to, of in pairs:
                sp.dma_start(to, of).then_inc(stored, 16)
            sp.wait_ge(stored, 16 * len(pairs))


def rows(table):
    return table.rearrange("(t p) f -> p t f", p=P)


def aggregate(nc, k, tag, table, idx, width, feat, attend=None):
    acc, dloc, d0i = k["acc"], k["dloc"], k["d0i"]
    with ExitStack() as s:
        def tb(name, shape, dt=fp32):
            return s.enter_context(nc.sbuf_tensor(f"{tag}_{name}", shape, dt))

        got = tb("got", [P, 2, U, width])
        slot = tb("slot", [P, 2, U], i32)
        sel = tb("sel", [P, 2, U, P])
        if attend is not None:
            msg = tb("msg", [P, 2, U, D])
            z = tb("z", [P, 2, U, NH])
            sj, real = attend
        part = s.enter_context(nc.psum_tensor(f"{tag}_part", [P, 2, U, P], fp32))
        names = ("got0", "got1", "slotted", "selected", "summed", "added", "scored", "exped", "exped_done", "ready", "passed")
        got0, got1, slotted, selected, summed, added, scored, exped, exped_done, ready, passed = s.enter_context(semaphores(nc, *names))
        arrived = (got0, got1)
        block = s.enter_context(nc.Block())

        @block.scalar
        def _(act):
            def stage(i, g):
                act.wait_ge(summed, i * 2 + (g + 1))
                nc.scalar.activation(slot[:, g], idx[:, bass.ds(i * G2 + g * U, U)], ACT.Copy).then_inc(slotted, 1)

            def exp(i, g):
                if attend is not None:
                    act.wait_ge(scored, i * 8 + (4 * g + 4))
                    nc.scalar.activation(z[:, g], z[:, g], ACT.Exp).then_inc(exped, 1)

            stage(0, 0)
            with act.Fori(0, STEPS - 1) as i:
                stage(i, 1)
                exp(i, 0)
                stage(i + 1, 0)
                exp(i, 1)
            stage(STEPS - 1, 1)
            exp(STEPS - 1, 0)
            exp(STEPS - 1, 1)

        @block.gpsimd
        def _(pool):
            pool.sem_inc(passed, 1)
            with pool.Fori(0, STEPS) as i:
                for g in range(2):
                    pool.wait_ge(summed, i * 2 + (g + 1))
                    pool.wait_ge(slotted, i * 2 + (g + 1))
                    pool.wait_ge(passed, i * 2 + (g + 1))
                    pass_gate(nc, k["gate"]).then_inc(passed, 1)
                    for u in range(U):
                        nc.gpsimd.indirect_dma_start(
                            got[:, g, u, :], None, table,
                            bass.IndirectOffsetOnAxis(ap=slot[:, g, u:u + 1], axis=0)).then_inc(arrived[g], 16)

        @block.tensor
        def _(pe):
            pe.sem_inc(summed, 2)
            with pe.Fori(0, STEPS) as i:
                for g in range(2):
                    pe.wait_ge(selected, i * 2 + (g + 1))
                    if attend is None:
                        pe.wait_ge(arrived[g], i * (16 * U) + 16 * U)
                    else:
                        pe.wait_ge(ready, i * 2 + (g + 1))
                    pe.wait_ge(added, i * (2 * U) + (g * U + U))
                    rows_of = got if attend is None else msg
                    for u in range(U):
                        last = nc.tensor.matmul(part[0:feat, g, u, :], rows_of[:, g, u, 0:feat], sel[:, g, u, :],
                                                start=True, stop=True)
                    last.then_inc(summed, 1)

        @block.vector
        def _(dve):
            v = nc.vector

            def front(i, g):
                j0 = i * G2 + g * U
                dve.wait_ge(summed, i * 2 + (g + 1))
                v.tensor_tensor(sel[:, g], k["iota_row"][:].unsqueeze(1).to_broadcast([P, U, P]),
                                dloc[:, bass.ds(j0, U)].unsqueeze(2).to_broadcast([P, U, P]), ALU.is_equal).then_inc(selected, 1)
                if attend is None:
                    return
                dve.wait_ge(arrived[g], i * (16 * U) + 16 * U)
                n = i * 8 + 4 * g
                v.tensor_tensor(z[:, g], got[:, g, :, D:D + NH], sj[:, bass.ds(j0, U), :], ALU.add).then_inc(scored, 1)
                dve.wait_ge(scored, n + 1)
                v.scalar_tensor_tensor(z[:, g], z[:, g], 0.2, z[:, g], ALU.mult, ALU.max).then_inc(scored, 1)
                dve.wait_ge(scored, n + 2)
                v.tensor_tensor(z[:, g], z[:, g], got[:, g, :, D + NH:D + 2 * NH], ALU.subtract).then_inc(scored, 1)
                dve.wait_ge(scored, n + 3)
                v.tensor_scalar(z[:, g], z[:, g], 0.0, None, ALU.min).then_inc(scored, 1)

            def weigh(i, g):
                j0 = i * G2 + g * U
                dve.wait_ge(exped, i * 2 + (g + 1))
                v.tensor_tensor(z[:, g], z[:, g], real[:, bass.ds(j0, U)].unsqueeze(2).to_broadcast([P, U, NH]),
                                ALU.mult).then_inc(exped_done, 1)
                dve.wait_ge(exped_done, i * 2 + (g + 1))
                v.tensor_tensor(msg[:, g].rearrange("p u (h c) -> p u h c", h=NH),
                                got[:, g, :, 0:D].rearrange("p u (h c) -> p u h c", h=NH),
                                z[:, g].unsqueeze(3).to_broadcast([P, U, NH, HC]), ALU.mult).then_inc(ready, 1)

            def add(i, g):
                _, at = nc.values_load_multi_w_load_instructions(
                    d0i[0:1, bass.ds(i * G2 + g * U, U)], engines=[mybir.EngineType.DVE], min_val=0, max_val=NP,
                    skip_runtime_bounds_check_because="destinations are nodes")
                dve.wait_ge(summed, i * 2 + (g + 3))
                for u in range(U):
                    dve.wait_ge(added, i * (2 * U) + (g * U + 2 * U + u))
                    w = acc[0:feat, bass.ds(at[u], P)]
                    v.tensor_tensor(w, w, part[0:feat, g, u, :], ALU.add).then_inc(added, 1)

            v.memset(acc[:], 0.0).then_inc(added, 2 * U)
            front(0, 0)
            if attend is not None:
                weigh(0, 0)
            with dve.Fori(0, STEPS - 1) as i:
                front(i, 1)
                add(i, 0)
                if attend is not None:
                    weigh(i, 1)
                front(i + 1, 0)
                add(i, 1)
                if attend is not None:
                    weigh(i + 1, 0)
            front(STEPS - 1, 1)
            add(STEPS - 1, 0)
            if attend is not None:
                weigh(STEPS - 1, 1)
            add(STEPS - 1, 1)


def load_all(nc, k):
    with ExitStack() as s:
        raw = s.enter_context(nc.sbuf_tensor("raw_w", [P, 3, D], fp32))
        pt = s.enter_context(nc.psum_tensor("turned_w", [P, 3, P], fp32))
        loaded, turned = s.enter_context(semaphores(nc, "loaded", "turned"))
        block = s.enter_context(nc.Block())
        w, brow, ball = k["w"], k["brow"], k["ball"]

        @block.sync
        def _(sp):
            loads = [(k["X"][:], rows(k["x"])), (w["0"][:], k["W0"]),
                     (w["att"][:, 0:NH], k["Watt"][0:D, :]), (w["att"][:, NH:2 * NH], k["Watt"][D:2 * D, :]),
                     (w["21"][:], k["W21"]), (w["22"][:], k["W22"]), (w["31"][:], k["W31"]), (w["32"][:], k["W32"]),
                     (brow[0:1, 0, :], k["b0"]), (brow[0:1, 1, :], k["bd"]), (brow[0:1, 2, :], k["bcn"]),
                     (brow[0:1, 3, :], k["bs"]), (k["batt_row"][0:1, 0:NH], k["batt"]),
                     (ball[:, 0, :], k["b21"].partition_broadcast(P).rearrange("p a d -> p (a d)")),
                     (ball[:, 1, :], k["b22"].partition_broadcast(P).rearrange("p a d -> p (a d)")),
                     (ball[:, 2, :], k["b32"].partition_broadcast(P).rearrange("p a d -> p (a d)")),
                     (k["b31_all"][:], k["b31"].partition_broadcast(P).rearrange("p a d -> p (a d)"))]
            loads += [(raw[:, n, :], k[m]) for n, m in enumerate(("Wd", "Wc", "Ws"))]
            for to, of in loads:
                sp.dma_start(to, of).then_inc(loaded, 16)
            sp.wait_ge(loaded, 16 * len(loads))

        @block.tensor
        def _(pe):
            pe.wait_ge(loaded, 16 * 20)
            for n in range(3):
                last = nc.tensor.transpose(pt[:, n, :], raw[:, n, :], k["ident"][:])
            last.then_inc(turned, 1)

        @block.vector
        def _(dve):
            nc.vector.memset(k["batt_row"][0:1, NH:2 * NH], 0.0)
            dve.wait_ge(turned, 1)
            for n in range(3):
                nc.vector.tensor_copy(w["1"][:, n, :], pt[:, n, :])


def attention_rows(nc, k, score, row8):
    H, acc, XL, count, offset = k["H"], k["acc"], k["XL"], k["count"], k["offset"]
    one_partition = lambda t: t.rearrange("(p j) f -> p j f", p=P)
    with ExitStack() as c:
        def sb(name, shape, dt=fp32):
            return c.enter_context(nc.sbuf_tensor("at_" + name, shape, dt))

        start = sb("start", [P, 2, NT], i32)
        end = sb("end", [P, NT], i32)
        f1, f2, node = sb("f1", [P, 2, NT]), sb("f2", [P, 2, NT]), sb("node", [P, 2, NT], i32)
        gathered = sb("gathered", [P, NT, NH])
        head_key = sb("head_key", [P, 1], i32)
        head = sb("head", [P, 2 * NH])
        gate = sb("gate", [P, J])
        fl = sb("fl", [P, J])

        with ExitStack() as s:
            iota_ready, steps = s.enter_context(semaphores(nc, "iota_ready", "steps"))
            block = s.enter_context(nc.Block())

            @block.gpsimd
            def _(pool):
                nc.gpsimd.iota(node[:], [[0, 2], [P, NT]], base=EP, channel_multiplier=1).then_inc(iota_ready, 1)

            @block.vector
            def _(dve):
                v, ch = nc.vector, Count(steps)
                ch.link(dve, v.tensor_scalar(f1[:], count[:], 0.0, None, ALU.is_equal))
                dve.wait_ge(iota_ready, 1)
                ch.link(dve, v.tensor_tensor(f2[:], node[:], offset[:], ALU.subtract))
                ch.link(dve, v.tensor_tensor(f2[:], f2[:], f1[:], ALU.mult))
                ch.link(dve, v.tensor_tensor(start[:], offset[:], f2[:], ALU.add))
                ch.link(dve, v.tensor_tensor(f1[:, 0], offset[:, 1], count[:, 1], ALU.add))
                ch.link(dve, v.tensor_scalar(end[:], f1[:, 0], -1.0, 0.0, ALU.add, ALU.max))
                ch.link(dve, v.memset(acc[:], 0.0))

        def indexed(tag, jobs):
            with ExitStack() as s:
                [moved] = s.enter_context(semaphores(nc, "moved"))
                block = s.enter_context(nc.Block())

                @block.gpsimd
                def _(pool):
                    for to, to_at, of, of_at in jobs:
                        nc.gpsimd.indirect_dma_start(
                            to, bass.IndirectOffsetOnAxis(ap=to_at, axis=0) if to_at is not None else None,
                            of, bass.IndirectOffsetOnAxis(ap=of_at, axis=0) if of_at is not None else None,
                        ).then_inc(moved, 16)
                    pool.wait_ge(moved, 16 * len(jobs))

        flat = k["row_start"].rearrange("r f -> (r f)").rearrange("(p q) -> p q", p=P)
        flat4 = k["sj_start"].rearrange("r f -> (r f)").rearrange("(p q) -> p q", p=P)
        w8, w4 = (EP + NP) * 2 * NH // P, (EP + NP) * NH // P
        store(nc, (rows(k["sj_node"]), score[:, :, NH:2 * NH]), (flat4, acc[:, 0:w4]),
              (flat[:, 0:w4], acc[:, 0:w4]), (flat[:, w4:w8], acc[:, 0:w8 - w4]))
        indexed("fill_dst", [(k["sj_start"], start[:, 0, t:t + 1], score[:, t, NH:2 * NH], None) for t in range(NT)])

        with ExitStack() as d:
            ed = d.enter_context(nc.sbuf_tensor("at_edges", [P, J, 4], fp32))
            pay = d.enter_context(nc.sbuf_tensor("at_pay", [P, J, 2 * NH], fp32))
            val = acc[:, 0:J * NH].rearrange("p (j h) -> p j h", h=NH)
            sje = H[:].rearrange("p t d -> p (t d)")[:, 0:J * NH].rearrange("p (j h) -> p j h", h=NH)
            with ExitStack() as s:
                loaded, keyed, moved, steps = s.enter_context(semaphores(nc, "loaded", "keyed", "moved", "steps"))
                block = s.enter_context(nc.Block())

                @block.sync
                def _(sp):
                    sp.dma_start(ed[:], one_partition(k["edges"])).then_inc(loaded, 16)
                    sp.dma_start(val, one_partition(k["sj_start"][0:EP, :])).then_inc(loaded, 16)

                @block.gpsimd
                def _(pool):
                    pool.wait_ge(keyed, 1)
                    nc.gpsimd.indirect_dma_start(head[:, 0:NH], None, k["sj_node"],
                                                 bass.IndirectOffsetOnAxis(ap=head_key[:], axis=0)).then_inc(moved, 16)

                @block.vector
                def _(dve):
                    v, ch = nc.vector, Count(steps)
                    dve.wait_ge(loaded, 32)
                    v.tensor_copy(head_key[:], ed[:, 0, 1:2]).then_inc(keyed, 1)
                    v.memset(gate[:, 0:1], 0.0)
                    v.memset(pay[:], 0.0)
                    ch.link(dve, v.tensor_tensor(gate[:, 1:J], ed[:, 1:J, 1], ed[:, 0:J - 1, 1], ALU.is_equal))
                    dve.wait_ge(moved, 16)
                    ch.link(dve, v.tensor_copy(val[:, 0, :], head[:, 0:NH]))
                    for h in range(NH):
                        ch.link(dve, v.tensor_tensor_scan(sje[:, :, h], gate[:], val[:, :, h], 0.0, ALU.mult, ALU.add))
                    v.tensor_copy(pay[:, :, 0:NH], sje)
                    ch.link(dve, v.tensor_scalar(fl[:], ed[:, :, 2], 2.0, float(LAST), ALU.is_equal, ALU.mult))
                    ch.link(dve, v.tensor_tensor(pay[:, :, NH], fl[:], ed[:, :, 0], ALU.max))

            with ExitStack() as s:
                slot = s.enter_context(nc.sbuf_tensor("at_slot", [P, 2, U], i32))
                row = s.enter_context(nc.sbuf_tensor("at_row", [P, 2, U, 2 * NH], fp32))
                stored, staged, out0, out1, passed = s.enter_context(
                    semaphores(nc, "stored", "staged", "out0", "out1", "passed"))
                moved = (out0, out1)
                block = s.enter_context(nc.Block())

                @block.sync
                def _(sp):
                    sp.dma_start(one_partition(k["sj_edge"]), sje).then_inc(stored, 16)
                    sp.wait_ge(stored, 16)

                @block.scalar
                def _(act):
                    with act.Fori(0, STEPS) as i:
                        for g in range(2):
                            act.wait_ge(moved[g], i * (16 * U) + 16)
                            a = bass.ds(i * G2 + g * U, U)
                            nc.scalar.activation(slot[:, g], ed[:, a, 3], ACT.Copy).then_inc(staged, 1)
                            nc.scalar.activation(row[:, g], pay[:, a, :], ACT.Copy).then_inc(staged, 1)

                @block.gpsimd
                def _(pool):
                    pool.sem_inc(passed, 1)
                    for g in range(2):
                        pool.dma_start(k["credit"][g:g + 1, :], k["gate"][:, 0:2]).then_inc(moved[g], 16)
                    with pool.Fori(0, STEPS) as i:
                        for g in range(2):
                            pool.wait_ge(staged, i * 4 + (2 * g + 2))
                            pool.wait_ge(passed, i * 2 + (g + 1))
                            pass_gate(nc, k["gate"]).then_inc(passed, 1)
                            for u in range(U):
                                nc.gpsimd.indirect_dma_start(
                                    k["by_src"], bass.IndirectOffsetOnAxis(ap=slot[:, g, u:u + 1], axis=0),
                                    row[:, g, u, :], None).then_inc(moved[g], 16)
                    for g in range(2):
                        pool.wait_ge(moved[g], STEPS * 16 * U + 16)

        with ExitStack() as d:
            by = d.enter_context(nc.sbuf_tensor("at_by", [P, J, 2 * NH], fp32))
            fill = d.enter_context(nc.sbuf_tensor("at_fill", [P, J, 2 * NH], fp32))
            before = d.enter_context(nc.sbuf_tensor("at_before", [P, 1], fp32))
            same = d.enter_context(nc.sbuf_tensor("at_same", [P, J], fp32))
            closed = d.enter_context(nc.sbuf_tensor("at_closed", [P, 2, NH], fp32))
            turned = d.enter_context(nc.sbuf_tensor("at_turned", [NH, 2, P], fp32))
            carry = d.enter_context(nc.sbuf_tensor("at_carry", [NH, P + 1], fp32))
            init = d.enter_context(nc.sbuf_tensor("at_init", [P, NH], fp32))
            psum = d.enter_context(nc.psum_tensor("at_ps", [P, 3, P], fp32))
            scan = acc[:, 0:J * NH].rearrange("p (j h) -> p j h", h=NH)
            val = H[:].rearrange("p t d -> p (t d)")[:, 0:J * NH].rearrange("p (j h) -> p j h", h=NH)

            def scan_over_partitions(tag, data, gates, op0, op1, none, pick, ready=None):
                with ExitStack() as s:
                    steps, ended, flipped, carried, back = s.enter_context(semaphores(nc, "steps", "ended", "flipped", "carried", "back"))
                    block = s.enter_context(nc.Block())

                    @block.tensor
                    def _(pe):
                        pe.wait_ge(ended, 1)
                        for n in range(2):
                            last = nc.tensor.transpose(psum[0:NH, n, :], closed[:, n, :], k["ident"][:])
                        last.then_inc(flipped, 1)
                        pe.wait_ge(carried, 1)
                        nc.tensor.transpose(psum[:, 2, 0:NH], carry[:, 0:P], k["ident"][0:NH, 0:NH]).then_inc(back, 1)

                    @block.vector
                    def _(dve):
                        v, ch = nc.vector, Count(steps)
                        for h in range(NH):
                            ch.link(dve, v.tensor_tensor_scan(scan[:, :, h], gates, data[:, :, h], none, op0, op1))
                        v.tensor_copy(closed[:, 0, :], scan[:, J - 1, :])
                        ch.link(dve, v.tensor_reduce(before[:], gates, AX.X, ALU.min))
                        v.tensor_copy(closed[:, 1, :], before[:].to_broadcast([P, NH])).then_inc(ended, 1)
                        ch.link(dve, v.memset(carry[:, 0:1], none))
                        dve.wait_ge(flipped, 1)
                        ch.link(dve, v.tensor_copy(turned[:], psum[0:NH, 0:2, :]))
                        v.tensor_tensor_scan(carry[:, 1:P + 1], turned[:, 1, :], turned[:, 0, :], none, op0, op1).then_inc(carried, 1)
                        dve.wait_ge(back, 1)
                        ch.link(dve, v.tensor_copy(init[:], psum[:, 2, 0:NH]))
                        for h in range(NH):
                            ch.link(dve, v.tensor_tensor_scan(scan[:, :, h], gates, data[:, :, h], init[:, h:h + 1], op0, op1))

            with ExitStack() as s:
                loaded, reset, steps = s.enter_context(semaphores(nc, "loaded", "reset", "steps"))
                block = s.enter_context(nc.Block())

                @block.sync
                def _(sp):
                    sp.dma_start(by[:], one_partition(k["by_src"])).then_inc(loaded, 16)
                    sp.wait_ge(reset, 1)
                    sp.dma_start(before[1:P, :], one_partition(k["by_src"])[0:P - 1, J - 1, NH:NH + 1],
                                 allow_slow_non_contiguous=True).then_inc(loaded, 16)

                @block.vector
                def _(dve):
                    v, ch = nc.vector, Count(steps)
                    v.memset(before[:], -1.0).then_inc(reset, 1)
                    dve.wait_ge(loaded, 32)
                    v.tensor_copy(head_key[:], by[:, 0, NH:NH + 1])
                    v.tensor_tensor(same[:, 0:1], by[:, 0, NH:NH + 1], before[:], ALU.is_equal)
                    ch.link(dve, v.tensor_tensor(same[:, 1:J], by[:, 1:J, NH], by[:, 0:J - 1, NH], ALU.is_equal))
                    ch.link(dve, v.tensor_scalar(fl[:], same[:], -1.0, BIG, ALU.add, ALU.mult))

            scan_over_partitions("max", by[:, :, 0:NH], fl[:], ALU.add, ALU.max, -BIG, None)
            store(nc, (one_partition(k["max_scan"]), scan))
            indexed("ends_max", [(gathered[:, t, :], None, k["max_scan"], end[:, t:t + 1]) for t in range(NT)])
            on_vector(nc, "max_rows",
                      lambda v: v.tensor_tensor(gathered[:], gathered[:], score[:, :, 0:NH], ALU.add),
                      lambda v: v.scalar_tensor_tensor(row8[:, :, NH:2 * NH], gathered[:], 0.2, gathered[:], ALU.mult, ALU.max),
                      lambda v: v.tensor_copy(row8[:, :, 0:NH], score[:, :, 0:NH]))
            store(nc, (rows(k["row_node"]), row8[:]))
            indexed("fill_src", [(k["row_start"], start[:, 1, t:t + 1], row8[:, t, :], None) for t in range(NT)]
                    + [(head[:], None, k["row_node"], head_key[:])])
            with ExitStack() as s:
                loaded, scored, exped, steps = s.enter_context(semaphores(nc, "loaded", "scored", "exped", "steps"))
                block = s.enter_context(nc.Block())

                @block.sync
                def _(sp):
                    sp.dma_start(fill[:], one_partition(k["row_start"][0:EP, :])).then_inc(loaded, 16)

                @block.vector
                def _(dve):
                    v, ch = nc.vector, Count(steps)
                    v.tensor_copy(gate[:], same[:])
                    ch.link(dve, v.memset(fl[:, 0:1], 0.0))
                    ch.link(dve, v.memset(gate[:, 0:1], 0.0))
                    dve.wait_ge(loaded, 16)
                    ch.link(dve, v.tensor_copy(fill[:, 0, :], head[:]))
                    for f in range(2 * NH):
                        ch.link(dve, v.tensor_tensor_scan(fill[:, :, f], gate[:], fill[:, :, f], 0.0, ALU.mult, ALU.add))
                    ch.link(dve, v.tensor_tensor(val, fill[:, :, 0:NH], by[:, :, 0:NH], ALU.add))
                    ch.link(dve, v.scalar_tensor_tensor(val, val, 0.2, val, ALU.mult, ALU.max))
                    v.tensor_tensor(val, val, fill[:, :, NH:2 * NH], ALU.subtract).then_inc(scored, 1)

                @block.scalar
                def _(act):
                    act.wait_ge(scored, 1)
                    nc.scalar.activation(val, val, ACT.Exp).then_inc(exped, 1)

            scan_over_partitions("sum", val, same[:], ALU.mult, ALU.add, 0.0, None)
            store(nc, (one_partition(k["sum_scan"]), scan))
            indexed("ends_sum", [(gathered[:, t, :], None, k["sum_scan"], end[:, t:t + 1]) for t in range(NT)])

        with ExitStack() as d:
            tab = d.enter_context(nc.sbuf_tensor("at_tab", [P, NT, AW], fp32))
            heads = lambda a: a.rearrange("p t (h c) -> p t h c", h=NH)
            on_vector(nc, "table0",
                      lambda v: v.tensor_scalar(gathered[:], gathered[:], 1e-16, None, ALU.add),
                      lambda v: v.reciprocal(gathered[:], gathered[:]),
                      *[lambda v, h=h: v.tensor_tensor(tab[:, :, h * HC:(h + 1) * HC], XL[:, :, h * HC:(h + 1) * HC],
                                                  gathered[:, :, h:h + 1].to_broadcast([P, NT, HC]), ALU.mult) for h in range(NH)],
                      lambda v: v.tensor_copy(tab[:, :, D:AW], row8[:]))
            store(nc, (rows(k["table0"]), tab[:]))


def layers(nc, k):
    X, H, acc, w, brow, ball, dinv = (k[n] for n in ("X", "H", "acc", "w", "brow", "ball", "dinv"))
    add_to = lambda to, got: nc.vector.tensor_tensor(to, to, got, ALU.add)
    wide = lambda t, n=D: t.unsqueeze(2).to_broadcast([P, NT, n])
    bias = lambda t, n=D: t.unsqueeze(1).to_broadcast([P, NT, n])

    layer_norm(nc, k, "ln0")
    with ExitStack() as s:
        XL = s.enter_context(nc.sbuf_tensor("XL", [P, NT, D], fp32))
        score = s.enter_context(nc.sbuf_tensor("score", [P, NT, 2 * NH], fp32))
        row8 = s.enter_context(nc.sbuf_tensor("row8", [P, NT, 2 * NH], fp32))
        node_loop(nc, k, "xl", H, XL, w["0"][:], brow[0:1, 0, :])
        node_loop(nc, k, "score", XL, score, w["att"][:], k["batt_row"][:], width=2 * NH)
        attention_rows(nc, k | {"XL": XL}, score, row8)
        on_vector(nc, "alone",
                  lambda v: v.tensor_tensor(XL[:], XL[:], wide(k["alone"][:]), ALU.mult),
                  lambda v: v.tensor_tensor(X[:], X[:], XL[:], ALU.add))
    with ExitStack() as s:
        sj = s.enter_context(nc.sbuf_tensor("sj_chunks", [P, J, NH], fp32))
        store(nc, (sj[:], k["sj_edge"].rearrange("(j p) f -> p j f", p=P)))
        aggregate(nc, k, "ag0", k["table0"], k["idx"], AW, D, attend=(sj, k["real"]))
    node_loop(nc, k, "out0", acc, X, take=add_to)

    layer_norm(nc, k, "ln1")
    for n in range(3):
        with ExitStack() as s:
            made = s.enter_context(nc.sbuf_tensor(f"made1{n}", [P, NT, D], fp32))
            node_loop(nc, k, f"m1{n}", H, made, w["1"][:, n, :], brow[0:1, 1 + n, :])
            store(nc, (rows(k["table1"][n * NP:(n + 1) * NP, :]), made[:]))
    aggregate(nc, k, "ag1", k["table1"], k["idx_typed"], D, D)
    node_loop(nc, k, "out1", acc, X,
              take=lambda to, got: nc.vector.scalar_tensor_tensor(to, got, 0.0, to, ALU.max, ALU.add))

    layer_norm(nc, k, "ln2")
    for n, c in enumerate("ab"):
        on_vector(nc, "scaled2" + c, lambda v: v.tensor_tensor(H[:], H[:], wide(dinv[:]), ALU.mult))
        store(nc, (rows(k["table2"][n]), H[:]))
        aggregate(nc, k, "ag2" + c, k["table2"][n], k["idx"], D, D)
        node_loop(nc, k, "out2" + c, acc, H, w[f"2{n + 1}"][:], turn=False)
        on_vector(nc, "relu2" + c,
                  lambda v: v.tensor_tensor(H[:], H[:], wide(dinv[:]), ALU.mult),
                  lambda v: v.tensor_tensor(H[:], H[:], bias(ball[:, n, :]), ALU.add),
                  lambda v: v.tensor_scalar(H[:], H[:], 0.0, None, ALU.max))
    on_vector(nc, "x3", lambda v: v.tensor_tensor(X[:], X[:], H[:], ALU.add))

    layer_norm(nc, k, "ln3")
    with ExitStack() as s:
        narrow = s.enter_context(nc.sbuf_tensor("narrow", [P, NT, D3], fp32))
        scaled = lambda v: v.tensor_tensor(narrow[:], narrow[:], wide(dinv[:], D3), ALU.mult)
        node_loop(nc, k, "in3", H, narrow, w["31"][:], width=D3)
        on_vector(nc, "scaled3a", scaled)
        store(nc, (rows(k["table3"][0]), narrow[:]))
        aggregate(nc, k, "ag3a", k["table3"][0], k["idx"], D3, D3)
        node_loop(nc, k, "out3a", acc, narrow, width=D3)
        on_vector(nc, "mid3", scaled,
                  lambda v: v.tensor_tensor(narrow[:], narrow[:], bias(k["b31_all"][:], D3), ALU.add), scaled)
        store(nc, (rows(k["table3"][1]), narrow[:]))
        aggregate(nc, k, "ag3b", k["table3"][1], k["idx"], D3, D3)
    node_loop(nc, k, "out3b", acc, H, w["32"][:], turn=False, feat=D3)
    on_vector(nc, "x4",
              lambda v: v.tensor_tensor(H[:], H[:], wide(dinv[:]), ALU.mult),
              lambda v: v.tensor_tensor(H[:], H[:], bias(ball[:, 2, :]), ALU.add),
              lambda v: v.tensor_scalar(H[:], H[:], 0.0, None, ALU.max),
              lambda v: v.tensor_tensor(X[:], X[:], H[:], ALU.add))
    full = (N // P) * P
    store(nc, (k["out"][0:full, :].rearrange("(t p) d -> p t d", p=P), X[:, 0:N // P, :]),
          (k["out"][full:N, :], X[0:N - full, N // P, :]))


_WEIGHTS = ["L0_gnn_W_lin", "L0_gnn_b_lin", "L0_gnn_W_att", "L0_gnn_b_att", "L1_gnn_W_data", "L1_gnn_b_data",
            "L1_gnn_W_control", "L1_gnn_b_control", "L1_gnn_W_self", "L1_gnn_b_self", "L2_gnn_W1", "L2_gnn_b1",
            "L2_gnn_W2", "L2_gnn_b2", "L3_gnn_W1", "L3_gnn_b1", "L3_gnn_W2", "L3_gnn_b2"]


def kernel(**inputs):
    import numpy as _np
    import concourse.bacc as _bacc
    from concourse import mybir as _mybir
    from concourse.bass_utils import run_bass_kernel_spmd as _run

    nodes = _np.arange(N, dtype=_np.int32)
    pads = _np.full(EP - E - N, N, _np.int32)

    def columns(*parts):
        return _np.ascontiguousarray(_np.concatenate([_np.asarray(a) for a in parts]).reshape(J, P).T)

    arrays = {
        "x": _np.concatenate([_np.asarray(inputs["x"]), _np.zeros((NP - N, D), _np.float32)]),
        "e_src": columns(inputs["src"], nodes, pads),
        "e_dst": columns(inputs["dst"], nodes, pads),
        "e_type": columns(inputs["edge_type_2"], _np.full(EP - E, 2, _np.int32)),
    }
    for name in _WEIGHTS:
        a = _np.ascontiguousarray(inputs[name])
        arrays[name] = a if a.ndim == 2 else a.reshape(1, -1)
    nc = _bacc.Bacc("TRN2", target_bir_lowering=False, num_devices=1)
    args = [nc.dram_tensor(n, a.shape, _mybir.dt.from_np(a.dtype), kind="ExternalInput").ap() for n, a in arrays.items()]
    out = nc.dram_tensor("out", (N, D), _mybir.dt.float32, kind="ExternalOutput").ap()
    gnn_kernel(nc, *args, out)
    r = _run(nc, [arrays], core_ids=[0])
    return r.results[0]["out"]
```

```python
import concourse.bass as bass
from concourse import mybir
from contextlib import ExitStack, contextmanager

fp32 = mybir.dt.float32
bf16 = mybir.dt.bfloat16
i32 = mybir.dt.int32
ALU = mybir.AluOpType
ACT = mybir.ActivationFunctionType
AX = mybir.AxisListType

P = 128
N = 6250
E = 106250
D = 128
NH, HC = 4, 32
D3 = 32
NT = (N + P - 1) // P
NP = NT * P
U = 8
G2 = 2 * U
STEPS = -(-(E + N) // (P * G2))
J = STEPS * G2
EP = J * P
LAST = NP - 1
AW = D + 2 * NH
BIG = 1e30
NG = 7
LN_EPS = 1e-5


def bc(ap, shape):
    return ap.to_broadcast(shape)


@contextmanager
def semaphores(nc, *names):
    sems = [nc.alloc_semaphore(f"{name}_{nc.next_id()}") for name in names]
    yield sems
    nc.clear_and_free_semaphores(sems)
    nc.all_engine_barrier()


class Count:

    def __init__(self, sem):
        self.sem, self.n = sem, 0

    def link(self, engine, ins):
        self.n += 1
        ins.then_inc(self.sem, 1)
        engine.wait_ge(self.sem, self.n)


def gnn_kernel(nc, x, e_src, e_dst, e_type, W0, b0, Watt, batt, Wd, bd, Wc, bcn, Ws, bs,
               W21, b21, W22, b22, W31, b31, W32, b32, out):
    ctx = ExitStack()

    credit = nc.dram_tensor("credit", (2, 2), fp32).ap()
    edges = nc.dram_tensor("edges_by_dst", (EP, 4), fp32).ap()
    sj_node = nc.dram_tensor("sj_node", (NP, NH), fp32).ap()
    sj_start = nc.dram_tensor("sj_start", (EP + NP, NH), fp32).ap()
    sj_edge = nc.dram_tensor("sj_edge", (EP, NH), fp32).ap()
    by_src = nc.dram_tensor("by_src", (EP, 2 * NH), fp32).ap()
    max_scan = nc.dram_tensor("max_scan", (EP, NH), fp32).ap()
    sum_scan = nc.dram_tensor("sum_scan", (EP, NH), fp32).ap()
    row_node = nc.dram_tensor("row_node", (NP, 2 * NH), fp32).ap()
    row_start = nc.dram_tensor("row_start", (EP + NP, 2 * NH), fp32).ap()
    table0 = nc.dram_tensor("table0", (NP, AW), fp32).ap()
    table1 = nc.dram_tensor("table1", (3 * NP, D), fp32).ap()
    table2 = [nc.dram_tensor(f"table2{c}", (NP, D), fp32).ap() for c in "ab"]
    table3 = [nc.dram_tensor(f"table3{c}", (NP, D3), fp32).ap() for c in "ab"]

    with ctx:
        def sb(name, shape, dt=fp32, c=ctx):
            return c.enter_context(nc.sbuf_tensor(name, shape, dt))

        X = sb("X", [P, NT, D])
        H = sb("H", [P, NT, D])
        acc = sb("acc", [P, NP + P])
        ident = sb("ident", [P, P])
        iota_row = sb("iota_row", [P, P])
        iota_col = sb("iota_col", [P, 1])
        ones = sb("ones", [P, P])
        above = sb("above", [P, P])
        zero_w = sb("zero_w", [P, P], bf16)
        gate = sb("gate", [1, 3])
        count = sb("count", [P, 2, NT])
        offset = sb("offset", [P, 2, NT])
        idx = sb("idx", [P, J], i32)
        idx_typed = sb("idx_typed", [P, J], i32)
        dloc = sb("dloc", [P, J])
        d0i = sb("d0i", [1, J], i32)
        cap = sb("cap", [P, J])
        dinv = sb("dinv", [P, NT])
        alone = sb("alone", [P, NT])
        w = {"0": sb("w0", [P, D]), "att": sb("watt", [P, 2 * NH]), "1": sb("w1", [P, 3, D]), "21": sb("w21", [P, D]),
             "22": sb("w22", [P, D]), "31": sb("w31", [P, D3]), "32": sb("w32", [D3, D])}
        brow = sb("brow", [1, 4, D])
        batt_row = sb("batt_row", [1, 2 * NH])
        ball = sb("ball", [P, 3, D])
        b31_all = sb("b31_all", [P, D3])

        sort_edges(nc, locals())
        edge_lists(nc, locals())
        load_all(nc, locals())
        layers(nc, locals())
    return


def sort_edges(nc, k):
    ident, iota_row, iota_col, ones, above = (k[n] for n in ("ident", "iota_row", "iota_col", "ones", "above"))
    count, offset, edges = k["count"], k["offset"], k["edges"]
    with ExitStack() as c:
        def sb(name, shape, dt=fp32):
            return c.enter_context(nc.sbuf_tensor(name, shape, dt))

        raw = sb("raw", [P, 3, J], i32)
        key = sb("key", [P, 2, J], i32)
        part = sb("part", [P, 2, J], i32)
        klo = sb("klo", [P, 2, J], bf16)
        khi = sb("khi", [P, 2, J], bf16)
        iota_i = sb("iota_i", [P, P + 1], i32)
        iota_b = sb("iota_b", [P, P], bf16)
        ident_b = sb("ident_b", [P, P], bf16)
        above_b = sb("above_b", [P, P], bf16)
        zeros = sb("zeros", [P, P], bf16)

        with ExitStack() as s:
            loaded, iota_ready, steps = s.enter_context(semaphores(nc, "loaded", "iota_ready", "steps"))
            block = s.enter_context(nc.Block())

            @block.sync
            def _(sp):
                for n, a in enumerate((k["e_src"], k["e_dst"], k["e_type"])):
                    sp.dma_start(raw[:, n, :], a).then_inc(loaded, 16)
                sp.wait_ge(loaded, 48)

            @block.gpsimd
            def _(pool):
                nc.gpsimd.iota(iota_i[:, 0:P], [[1, P]], base=0, channel_multiplier=0).then_inc(iota_ready, 1)
                nc.gpsimd.iota(iota_i[:, P:P + 1], [[1, 1]], base=0, channel_multiplier=1).then_inc(iota_ready, 1)

            @block.vector
            def _(dve):
                v, ch = nc.vector, Count(steps)
                v.memset(ones[:], 1.0)
                v.memset(zeros[:], 0.0)
                v.memset(k["zero_w"][:], 0.0)
                v.memset(k["gate"][:], 0.0)
                dve.wait_ge(iota_ready, 2)
                v.tensor_copy(iota_row[:], iota_i[:, 0:P])
                ch.link(dve, v.tensor_copy(iota_col[:], iota_i[:, P:P + 1]))
                v.tensor_copy(iota_b[:], iota_row[:])
                v.tensor_scalar(ident[:], iota_row[:], iota_col[:, 0:1], None, ALU.is_equal)
                v.tensor_scalar(above[:], iota_row[:], iota_col[:, 0:1], None, ALU.is_gt)
                v.tensor_scalar(ident_b[:], iota_row[:], iota_col[:, 0:1], None, ALU.is_equal)
                v.tensor_scalar(above_b[:], iota_row[:], iota_col[:, 0:1], None, ALU.is_gt)
                dve.wait_ge(loaded, 48)
                v.tensor_copy(key[:, 0, :], raw[:, 1, :])
                ch.link(dve, v.tensor_scalar(key[:, 1, :], raw[:, 2, :], 2.0, float(LAST), ALU.is_equal, ALU.mult))
                ch.link(dve, v.tensor_tensor(key[:, 1, :], key[:, 1, :], raw[:, 0, :], ALU.max))
                ch.link(dve, v.tensor_scalar(part[:], key[:], P - 1, None, ALU.bitwise_and))
                ch.link(dve, v.tensor_copy(klo[:], part[:]))
                ch.link(dve, v.tensor_scalar(part[:], key[:], 7, None, ALU.logical_shift_right))
                ch.link(dve, v.tensor_copy(khi[:], part[:]))

        def one_hots(dve, lo, hi, keys, j0):
            n = len(keys)
            a, b = keys[0], keys[-1] + 1
            nc.vector.tensor_tensor(
                lo, iota_b[:].unsqueeze(1).unsqueeze(1).to_broadcast([P, n, U, P]),
                klo[:, a:b, bass.ds(j0, U)].unsqueeze(3).to_broadcast([P, n, U, P]), ALU.is_equal)
            return nc.vector.tensor_tensor(
                hi, iota_b[:, 0:NT].unsqueeze(1).unsqueeze(1).to_broadcast([P, n, U, NT]),
                khi[:, a:b, bass.ds(j0, U)].unsqueeze(3).to_broadcast([P, n, U, NT]), ALU.is_equal)

        with ExitStack() as s:
            lo = s.enter_context(nc.sbuf_tensor("lo", [P, 2, 2, U, P], bf16))
            hi = s.enter_context(nc.sbuf_tensor("hi", [P, 2, 2, U, NT], bf16))
            hist = [s.enter_context(nc.psum_tensor(f"hist{n}", [P, 512], fp32)) for n in range(2)]
            prefix = s.enter_context(nc.psum_tensor("prefix", [P, 2, 2, NT], fp32))
            zero_row = s.enter_context(nc.sbuf_tensor("zero_row", [P, NT], fp32))
            incl = s.enter_context(nc.sbuf_tensor("incl", [P, 2, NT], fp32))
            built, used, counted, copied, summed, steps = s.enter_context(semaphores(nc, "built", "used", "counted", "copied", "summed", "steps"))
            block = s.enter_context(nc.Block())

            @block.vector
            def _(dve):
                v, ch = nc.vector, Count(steps)
                v.memset(zero_row[:], 0.0)
                with dve.Fori(0, STEPS) as i:
                    for g in range(2):
                        dve.wait_ge(used, i * 2 + (g + 1))
                        one_hots(dve, lo[:, g], hi[:, g], (0, 1), i * G2 + g * U).then_inc(built, 1)
                dve.wait_ge(counted, 1)
                for n in range(2):
                    last = v.tensor_copy(count[:, n, :], hist[n][:, 0:NT])
                last.then_inc(copied, 1)
                dve.wait_ge(summed, 1)
                for n in range(2):
                    ch.link(dve, v.tensor_tensor_scan(incl[:, n, :], prefix[:, 1, n, :], zero_row[:], 0.0, ALU.add, ALU.add))
                ch.link(dve, v.tensor_tensor(incl[:], incl[:], prefix[:, 1], ALU.subtract))
                ch.link(dve, v.tensor_tensor(offset[:], incl[:], prefix[:, 0], ALU.add))

            @block.tensor
            def _(pe):
                for n in range(2):
                    last = nc.tensor.matmul(hist[n][:, 0:NT], zeros[:], zeros[:, 0:NT], start=True, stop=False)
                last.then_inc(used, 2)
                with pe.Fori(0, STEPS) as i:
                    for g in range(2):
                        pe.wait_ge(built, i * 2 + (g + 1))
                        for n in range(2):
                            for u in range(U):
                                last = nc.tensor.matmul(hist[n][:, 0:NT], lo[:, g, n, u, :], hi[:, g, n, u, :],
                                                        start=False, stop=False)
                        last.then_inc(used, 1)
                for n in range(2):
                    last = nc.tensor.matmul(hist[n][:, 0:NT], zeros[:], zeros[:, 0:NT], start=False, stop=True)
                last.then_inc(counted, 1)
                pe.wait_ge(copied, 1)
                for n in range(2):
                    nc.tensor.matmul(prefix[:, 0, n, :], above[:], count[:, n, :], start=True, stop=True)
                    last = nc.tensor.matmul(prefix[:, 1, n, :], ones[:], count[:, n, :], start=True, stop=True)
                last.then_inc(summed, 1)

        with ExitStack() as s:
            def tb(name, shape, dt=fp32):
                return s.enter_context(nc.sbuf_tensor("place_" + name, shape, dt))

            lo = tb("lo", [P, 2, 2, U, P], bf16)
            hi = tb("hi", [P, 2, 2, U, NT], bf16)
            loT = tb("loT", [P, 2, 2, U, P])
            apart = tb("apart", [P, U, P], bf16)
            same = tb("same", [P, 2, 2, U, P], bf16)
            base = tb("base", [P, 2, 2, U, NT])
            stage = tb("stage", [P, 2, U], bf16)
            picked = tb("picked", [P, 2, U, NT])
            placef = tb("placef", [P, 2, U])
            place = tb("place", [P, 2, U], i32)
            row = tb("row", [P, 2, U, 4])
            minus = tb("minus", [P, 1])
            penalty = tb("penalty", [P, P], bf16)
            lorow = [s.enter_context(nc.psum_tensor(f"lorow{n}", [P, U, P], bf16)) for n in range(2)]
            masked = s.enter_context(nc.psum_tensor("masked", [P, U, P], fp32))
            cum = [s.enter_context(nc.psum_tensor(f"cum{n}", [P, U, 64], fp32)) for n in range(2)]
            look = [s.enter_context(nc.psum_tensor(f"look{n}", [P, U, 64], fp32)) for n in range(2)]
            (staged, spread, barred, absed, turned, matched, hot, cummed, stepped, based, looked, weighed, placed, rowed,
             scat0, scat1, passed, ready, summed) = s.enter_context(semaphores(
                 nc, "staged", "spread", "barred", "absed", "turned", "matched", "hot", "cummed", "stepped", "based",
                 "looked", "weighed", "placed", "rowed", "scat0", "scat1", "passed", "ready", "summed"))
            scattered = (scat0, scat1)
            block = s.enter_context(nc.Block())

            def over_groups(engine, before, main):
                before(0, 0)
                with engine.Fori(0, STEPS - 1) as i:
                    for g in range(2):
                        main(i, g, (i, 1) if g == 0 else (i + 1, 0))
                main(STEPS - 1, 0, (STEPS - 1, 1))
                main(STEPS - 1, 1, None)

            @block.scalar
            def _(act):
                def turn(i, g):
                    for n in range(2):
                        m = i * 4 + (2 * g + n)
                        act.wait_ge(spread, m + 1)
                        act.wait_ge(turned, m + 2)
                        nc.scalar.activation(apart[:], lorow[n][:], ACT.Abs, bias=minus[:, 0:1]).then_inc(absed, 1)
                        act.wait_ge(absed, m + 1)
                        act.wait_ge(looked, m + 1)
                        nc.scalar.activation(loT[:, g, n], apart[:], ACT.Relu, bias=k["ones"][:, 0:1],
                                             scale=-1.0).then_inc(turned, 1)

                def before(i, g):
                    nc.scalar.activation(stage[:], klo[:, :, bass.ds(i * G2 + g * U, U)], ACT.Copy).then_inc(staged, 1)
                    turn(i, g)

                def main(i, g, ahead):
                    act.wait_ge(scattered[g], i * (16 * U) + 16)
                    nc.scalar.activation(row[:, g, :, 0:3], raw[:, :, bass.ds(i * G2 + g * U, U)].rearrange("p f u -> p u f"),
                                         ACT.Copy).then_inc(rowed, 1)
                    if ahead is not None:
                        act.wait_ge(barred, i * 4 + (2 * g + 2))
                        before(*ahead)

                act.sem_inc(turned, 2)
                act.wait_ge(ready, 1)
                over_groups(act, before, main)

            @block.tensor
            def _(pe):
                def spread_out(i, g, n):
                    m = i * 4 + (2 * g + n)
                    pe.wait_ge(staged, i * 2 + (g + 1))
                    pe.wait_ge(turned, m + 1)
                    for u in range(U):
                        last = nc.tensor.transpose(lorow[n][:, u, :], stage[:, n, u:u + 1].to_broadcast([P, P]), ident_b[:])
                    last.then_inc(spread, 1)
                    pe.wait_ge(matched, m + 1)
                    for v0 in range(0, U, 4):
                        nc.tensor.matmul(masked[:, v0:v0 + 4, :], ident_b[:], penalty[:].unsqueeze(1).to_broadcast([P, 4, P]),
                                         start=True, stop=False)
                        for u in range(v0, v0 + 4):
                            last = nc.tensor.matmul(masked[:, u, :], stage[:, n, u:u + 1].to_broadcast([P, P]), ident_b[:],
                                                    start=False, stop=u == v0 + 3)
                    last.then_inc(barred, 1)

                def add_up(i, g, n):
                    m = i * 4 + (2 * g + n)
                    pe.wait_ge(hot, m + 1)
                    pe.wait_ge(based, m + 1)
                    for v0 in range(0, U, 4):
                        for u in range(v0, v0 + 4):
                            for w in range(v0, u + 1):
                                last = nc.tensor.matmul(cum[n][:, u, 0:NT], lo[:, g, n, w, :], hi[:, g, n, w, :],
                                                        start=w == v0, stop=w == u)
                    last.then_inc(cummed, 1)

                def look_up(i, g, n):
                    m = i * 4 + (2 * g + n)
                    pe.wait_ge(based, m + 3)
                    pe.wait_ge(turned, m + 3)
                    pe.wait_ge(weighed, m + 1)
                    for u in range(U):
                        nc.tensor.matmul(look[n][:, u, 0:NT], loT[:, g, n, u, :],
                                         base[:, g, n, u - 1, :] if u else base[:, 1 - g, n, U - 1, :], start=True, stop=False)
                        last = nc.tensor.matmul(look[n][:, u, 0:NT], same[:, g, n, u, :], hi[:, g, n, u, :], start=False, stop=True)
                    last.then_inc(looked, 1)

                def before(i, g):
                    for n in range(2):
                        spread_out(i, g, n)

                def main(i, g, ahead):
                    for n in range(2):
                        add_up(i, g, n)
                    for n in range(2):
                        if ahead is not None:
                            spread_out(*ahead, n)
                        look_up(i, g, n)

                pe.sem_inc(looked, 4)
                pe.wait_ge(ready, 1)
                over_groups(pe, before, main)

            @block.vector
            def _(dve):
                v = nc.vector

                def before(i, g):
                    j0 = i * G2 + g * U
                    for n in range(2):
                        m = i * 4 + (2 * g + n)
                        dve.wait_ge(barred, m + 1)
                        dve.wait_ge(looked, m + 1)
                        v.tensor_tensor(same[:, g, n], masked[:], klo[:, n, bass.ds(j0, U)].unsqueeze(2).to_broadcast([P, U, P]),
                                        ALU.is_equal).then_inc(matched, 1)
                        one_hots(dve, lo[:, g, n:n + 1], hi[:, g, n:n + 1], (n,), j0).then_inc(hot, 1)

                def main(i, g, ahead):
                    for n in range(2):
                        m = i * 4 + (2 * g + n)
                        dve.wait_ge(cummed, m + 1)
                        dve.wait_ge(based, m + 1)
                        v.tensor_tensor(base[:, g, n, 0:4, :], cum[n][:, 0:4, 0:NT],
                                        base[:, 1 - g, n, U - 1:U, :].to_broadcast([P, 4, NT]), ALU.add).then_inc(stepped, 1)
                        dve.wait_ge(stepped, m + 1)
                        v.tensor_tensor(base[:, g, n, 4:8, :], cum[n][:, 4:8, 0:NT],
                                        base[:, g, n, 3:4, :].to_broadcast([P, 4, NT]), ALU.add).then_inc(based, 1)
                    if ahead is not None:
                        before(*ahead)
                    for n in range(2):
                        m = i * 4 + (2 * g + n)
                        dve.wait_ge(looked, m + 5)
                        v.tensor_tensor(picked[:, n], look[n][:, :, 0:NT], hi[:, g, n], ALU.mult).then_inc(weighed, 1)
                        dve.wait_ge(weighed, m + 3)
                        dve.wait_ge(scattered[g], i * (16 * U) + 16)
                        v.tensor_reduce(placef[:, g] if n == 0 else row[:, g, :, 3], picked[:, n], AX.X,
                                        ALU.add).then_inc(summed, 1)
                    dve.wait_ge(summed, i * 4 + (2 * g + 1))
                    v.tensor_copy(place[:, g], placef[:, g]).then_inc(placed, 1)

                v.tensor_copy(base[:, 1, :, U - 1, :], offset[:]).then_inc(based, 2)
                v.tensor_scalar(penalty[:], above[:], -512.0, 512.0, ALU.mult, ALU.add)
                v.tensor_scalar(minus[:], iota_col[:], -1.0, None, ALU.mult).then_inc(ready, 1)
                dve.sem_inc(matched, 1)
                dve.sem_inc(weighed, 2)
                over_groups(dve, before, main)

            @block.gpsimd
            def _(pool):
                for g in range(2):
                    pool.dma_start(k["credit"][g:g + 1, :], k["gate"][:, 0:2]).then_inc(scattered[g], 16)
                with pool.Fori(0, STEPS) as i:
                    for g in range(2):
                        pool.wait_ge(rowed, i * 2 + (g + 1))
                        pool.wait_ge(placed, i * 2 + (g + 1))
                        pool.sem_inc(passed, 1)
                        for u in range(U):
                            nc.gpsimd.indirect_dma_start(
                                edges, bass.IndirectOffsetOnAxis(ap=place[:, g, u:u + 1], axis=0),
                                row[:, g, u, :], None).then_inc(scattered[g], 16)
                for g in range(2):
                    pool.wait_ge(scattered[g], STEPS * 16 * U + 16)


def edge_lists(nc, k):
    idx, idx_typed, dloc, d0i, cap = (k[n] for n in ("idx", "idx_typed", "dloc", "d0i", "cap"))
    with ExitStack() as s:
        es = s.enter_context(nc.sbuf_tensor("sorted_chunks", [P, J, 4], fp32))
        d0 = s.enter_context(nc.sbuf_tensor("first_dst", [1, J], fp32))
        root = s.enter_context(nc.sbuf_tensor("root", [P, NT], fp32))
        first = s.enter_context(nc.psum_tensor("first_all", [P, 2, 512], fp32))
        loaded, firsts, spread, rooted, rooting, steps = s.enter_context(semaphores(nc, "loaded", "firsts", "spread", "rooted", "rooting", "steps"))
        block = s.enter_context(nc.Block())
        half = J // 2

        @block.sync
        def _(sp):
            sp.dma_start(es[:], k["edges"].rearrange("(j p) f -> p j f", p=P)).then_inc(loaded, 16)

        @block.vector
        def _(dve):
            v, ch = nc.vector, Count(steps)
            ch.link(dve, v.tensor_scalar(root[:], k["count"][:, 0, :], 1.0, None, ALU.max))
            v.tensor_scalar(k["alone"][:], root[:], 1.0, None, ALU.is_equal).then_inc(rooting, 1)
            dve.wait_ge(loaded, 16)
            v.tensor_copy(d0i[:], es[0:1, :, 1])
            v.tensor_copy(d0[:], es[0:1, :, 1]).then_inc(firsts, 1)
            v.tensor_copy(idx[:], es[:, :, 0])
            v.tensor_scalar(cap[:], es[:, :, 2], 2.0, -BIG, ALU.is_equal, ALU.mult)
            v.scalar_tensor_tensor(idx_typed[:], es[:, :, 2], float(NP), es[:, :, 0], ALU.mult, ALU.add)
            dve.wait_ge(spread, 1)
            for n in range(2):
                a = slice(n * half, (n + 1) * half)
                v.tensor_tensor(dloc[:, a], es[:, a, 1], first[:, n, 0:half], ALU.subtract)
            dve.wait_ge(rooted, 1)
            v.reciprocal(k["dinv"][:], root[:])

        @block.scalar
        def _(act):
            act.wait_ge(rooting, 1)
            nc.scalar.activation(root[:], root[:], ACT.Sqrt).then_inc(rooted, 1)

        @block.tensor
        def _(pe):
            pe.wait_ge(firsts, 1)
            for n in range(2):
                last = nc.tensor.matmul(first[:, n, 0:half], k["ones"][0:1, :], d0[0:1, n * half:(n + 1) * half],
                                        start=True, stop=True)
            last.then_inc(spread, 1)


def layer_norm(nc, k, tag):
    X, H = k["X"], k["H"]
    with ExitStack() as s:
        stat = s.enter_context(nc.sbuf_tensor(tag + "_stat", [P, NT], fp32))
        rstd = s.enter_context(nc.sbuf_tensor(tag + "_rstd", [P, NT], fp32))
        square = k["acc"][:, 0:NP].rearrange("p (t d) -> p t d", d=D)
        steps, squared, spread, rooted = s.enter_context(semaphores(nc, "steps", "squared", "spread", "rooted"))
        block = s.enter_context(nc.Block())
        wide = lambda t: t[:].unsqueeze(2).to_broadcast([P, NT, D])

        @block.vector
        def _(dve):
            v, ch = nc.vector, Count(steps)
            ch.link(dve, v.tensor_reduce(stat[:], X[:], AX.X, ALU.add))
            ch.link(dve, v.tensor_scalar(stat[:], stat[:], 1.0 / D, None, ALU.mult))
            v.tensor_tensor(H[:], X[:], wide(stat), ALU.subtract).then_inc(spread, 1)
            dve.wait_ge(squared, 1)
            ch.link(dve, v.tensor_reduce(stat[:], square, AX.X, ALU.add))
            v.tensor_scalar(stat[:], stat[:], 1.0 / D, LN_EPS, ALU.mult, ALU.add).then_inc(spread, 1)
            dve.wait_ge(rooted, 1)
            ch.link(dve, v.reciprocal(rstd[:], stat[:]))
            ch.link(dve, v.tensor_tensor(H[:], H[:], wide(rstd), ALU.mult))
            v.tensor_scalar(H[:], H[:], 0.0, None, ALU.max)

        @block.scalar
        def _(act):
            act.wait_ge(spread, 1)
            nc.scalar.activation(square, H[:], ACT.Square).then_inc(squared, 1)
            act.wait_ge(spread, 2)
            nc.scalar.activation(stat[:], stat[:], ACT.Sqrt).then_inc(rooted, 1)


def node_loop(nc, k, tag, source, dest, weight=None, bias=None, turn=True, feat=D, width=D, take=None):
    ident, ones = k["ident"], k["ones"]
    flat = len(source.shape) == 2
    with ExitStack() as s:
        turned = s.enter_context(nc.sbuf_tensor(tag + "_turned", [P, NG, P], fp32))
        pt = s.enter_context(nc.psum_tensor(tag + "_pt", [P, NG + 1, P], fp32))
        pm = s.enter_context(nc.psum_tensor(tag + "_pm", [P, NG + 1, P], fp32))
        tiles = s.enter_context(nc.sbuf_tensor(tag + "_tiles", [P, NG, P], fp32))
        staged, flipped, kept, made, taken = s.enter_context(
            semaphores(nc, "staged", "flipped", "kept", "made", "taken"))
        block = s.enter_context(nc.Block())
        rows_in = feat if flat else P
        read = flipped if turn else made

        @block.scalar
        def _(act):
            act.sem_inc(kept, 1)
            with act.Fori(0, NT // NG) as i:
                act.wait_ge(read, i + 1)
                of = source[0:feat, bass.ds(i * (NG * P), NG * P)] if flat else \
                    source[:, bass.ds(i * NG, NG), :].rearrange("p t d -> p (t d)")
                nc.scalar.activation(tiles[0:rows_in].rearrange("p t d -> p (t d)"), of, ACT.Copy).then_inc(staged, 1)
                if turn and weight is not None:
                    act.wait_ge(flipped, i + 2)
                    act.wait_ge(made, i + 1)
                    nc.scalar.activation(turned[:], pt[:, 0:NG, :], ACT.Copy).then_inc(kept, 1)

        @block.tensor
        def _(pe):
            pe.sem_inc(flipped, 1)
            pe.sem_inc(made, 1)
            with pe.Fori(0, NT // NG) as i:
                pe.wait_ge(staged, i + 1)
                if turn:
                    pe.wait_ge(kept if weight is not None else taken, i + 1)
                    for u in range(NG):
                        last = nc.tensor.transpose(pt[:, u, 0:rows_in], tiles[0:rows_in, u, :], ident[0:rows_in, 0:rows_in])
                    last.then_inc(flipped, 1)
                if weight is not None:
                    if turn:
                        pe.wait_ge(kept, i + 2)
                    pe.wait_ge(taken, i + 1)
                    for u in range(NG):
                        lhs = turned[:, u, :] if turn else tiles[0:rows_in, u, :]
                        last = nc.tensor.matmul(pm[:, u, 0:width], lhs, weight, start=True, stop=bias is None)
                        if bias is not None:
                            last = nc.tensor.matmul(pm[:, u, 0:width], ones[0:1, :], bias, start=False, stop=True)
                    last.then_inc(made, 1)

        @block.vector
        def _(dve):
            dve.sem_inc(taken, 1)
            with dve.Fori(0, NT // NG) as i:
                dve.wait_ge(made if weight is not None else flipped, i + 2)
                got = (pm if weight is not None else pt)[:, 0:NG, 0:width]
                to = dest[:, bass.ds(i * NG, NG), 0:width]
                if take is None:
                    nc.vector.tensor_copy(to, got).then_inc(taken, 1)
                else:
                    take(to, got).then_inc(taken, 1)


def on_vector(nc, tag, *ops):
    with ExitStack() as s:
        [steps] = s.enter_context(semaphores(nc, "steps"))
        block = s.enter_context(nc.Block())

        @block.vector
        def _(dve):
            ch = Count(steps)
            for op in ops:
                ch.link(dve, op(nc.vector))


def store(nc, *pairs):
    with ExitStack() as s:
        [stored] = s.enter_context(semaphores(nc, "stored"))
        block = s.enter_context(nc.Block())

        @block.sync
        def _(sp):
            for to, of in pairs:
                sp.dma_start(to, of).then_inc(stored, 16)
            sp.wait_ge(stored, 16 * len(pairs))


def rows(table):
    return table.rearrange("(t p) f -> p t f", p=P)


def aggregate(nc, k, tag, table, idx, width, feat, attend=None):
    acc, dloc, d0i = k["acc"], k["dloc"], k["d0i"]
    with ExitStack() as s:
        def tb(name, shape, dt=fp32):
            return s.enter_context(nc.sbuf_tensor(f"{tag}_{name}", shape, dt))

        got = tb("got", [P, 2, U, width])
        slot = tb("slot", [P, 2, U], i32)
        sel = tb("sel", [P, 2, U, P])
        if attend is not None:
            msg = tb("msg", [P, 2, U, D])
            z = tb("z", [P, 2, U, NH])
            sj, cap = attend
        part = s.enter_context(nc.psum_tensor(f"{tag}_part", [P, 2, U, P], fp32))
        names = ("got0", "got1", "slotted", "selected", "summed", "added", "scored", "exped", "ready", "passed")
        got0, got1, slotted, selected, summed, added, scored, exped, ready, passed = s.enter_context(semaphores(nc, *names))
        arrived = (got0, got1)
        used = summed if attend is None else ready
        block = s.enter_context(nc.Block())

        @block.scalar
        def _(act):
            def stage(i, g):
                act.wait_ge(used, i * 2 + (g + 1))
                nc.scalar.activation(slot[:, g], idx[:, bass.ds(i * G2 + g * U, U)], ACT.Copy).then_inc(slotted, 1)

            def exp(i, g):
                if attend is not None:
                    act.wait_ge(scored, i * 8 + (4 * g + 4))
                    nc.scalar.activation(z[:, g], z[:, g], ACT.Exp).then_inc(exped, 1)

            stage(0, 0)
            with act.Fori(0, STEPS - 1) as i:
                stage(i, 1)
                exp(i, 0)
                stage(i + 1, 0)
                exp(i, 1)
            stage(STEPS - 1, 1)
            exp(STEPS - 1, 0)
            exp(STEPS - 1, 1)

        @block.gpsimd
        def _(pool):
            with pool.Fori(0, STEPS) as i:
                for g in range(2):
                    pool.wait_ge(used, i * 2 + (g + 1))
                    pool.wait_ge(slotted, i * 2 + (g + 1))
                    pool.sem_inc(passed, 1)
                    for u in range(U):
                        nc.gpsimd.indirect_dma_start(
                            got[:, g, u, :], None, table,
                            bass.IndirectOffsetOnAxis(ap=slot[:, g, u:u + 1], axis=0)).then_inc(arrived[g], 16)

        @block.tensor
        def _(pe):
            pe.sem_inc(summed, 2)
            with pe.Fori(0, STEPS) as i:
                for g in range(2):
                    pe.wait_ge(selected, i * 2 + (g + 1))
                    if attend is None:
                        pe.wait_ge(arrived[g], i * (16 * U) + 16 * U)
                    else:
                        pe.wait_ge(ready, i * 2 + (g + 3))
                    pe.wait_ge(added, i * (2 * U) + (g * U + U))
                    rows_of = got if attend is None else msg
                    for u in range(U):
                        last = nc.tensor.matmul(part[0:feat, g, u, :], rows_of[:, g, u, 0:feat], sel[:, g, u, :],
                                                start=True, stop=True)
                    last.then_inc(summed, 1)

        @block.vector
        def _(dve):
            v = nc.vector

            def front(i, g):
                j0 = i * G2 + g * U
                dve.wait_ge(summed, i * 2 + (g + 1))
                v.tensor_tensor(sel[:, g], k["iota_row"][:].unsqueeze(1).to_broadcast([P, U, P]),
                                dloc[:, bass.ds(j0, U)].unsqueeze(2).to_broadcast([P, U, P]), ALU.is_equal).then_inc(selected, 1)
                if attend is None:
                    return
                dve.wait_ge(arrived[g], i * (16 * U) + 16 * U)
                n = i * 8 + 4 * g
                v.tensor_tensor(z[:, g], got[:, g, :, D:D + NH], sj[:, bass.ds(j0, U), :], ALU.add).then_inc(scored, 1)
                dve.wait_ge(scored, n + 1)
                v.scalar_tensor_tensor(z[:, g], z[:, g], 0.2, z[:, g], ALU.mult, ALU.max).then_inc(scored, 1)
                dve.wait_ge(scored, n + 2)
                v.tensor_tensor(z[:, g], z[:, g], got[:, g, :, D + NH:D + 2 * NH], ALU.subtract).then_inc(scored, 1)
                dve.wait_ge(scored, n + 3)
                v.tensor_tensor(z[:, g], z[:, g], cap[:, bass.ds(j0, U)].unsqueeze(2).to_broadcast([P, U, NH]),
                                ALU.min).then_inc(scored, 1)
                dve.wait_ge(exped, i * 2 + (g + 1))
                v.tensor_tensor(msg[:, g].rearrange("p u (h c) -> p u h c", h=NH),
                                got[:, g, :, 0:D].rearrange("p u (h c) -> p u h c", h=NH),
                                z[:, g].unsqueeze(3).to_broadcast([P, U, NH, HC]), ALU.mult).then_inc(ready, 1)

            def add(i, g):
                _, at = nc.values_load_multi_w_load_instructions(
                    d0i[0:1, bass.ds(i * G2 + g * U, U)], engines=[mybir.EngineType.DVE], min_val=0, max_val=NP,
                    skip_runtime_bounds_check_because="destinations are nodes")
                dve.wait_ge(summed, i * 2 + (g + 3))
                for u in range(U):
                    dve.wait_ge(added, i * (2 * U) + (g * U + 2 * U + u))
                    w = acc[0:feat, bass.ds(at[u], P)]
                    v.tensor_tensor(w, w, part[0:feat, g, u, :], ALU.add).then_inc(added, 1)

            v.memset(acc[:], 0.0).then_inc(added, 2 * U)
            if attend is not None:
                dve.sem_inc(ready, 2)
            front(0, 0)
            with dve.Fori(0, STEPS - 1) as i:
                front(i, 1)
                add(i, 0)
                front(i + 1, 0)
                add(i, 1)
            front(STEPS - 1, 1)
            add(STEPS - 1, 0)
            add(STEPS - 1, 1)


def load_all(nc, k):
    with ExitStack() as s:
        raw = s.enter_context(nc.sbuf_tensor("raw_w", [P, 3, D], fp32))
        pt = s.enter_context(nc.psum_tensor("turned_w", [P, 3, P], fp32))
        loaded, turned = s.enter_context(semaphores(nc, "loaded", "turned"))
        block = s.enter_context(nc.Block())
        w, brow, ball = k["w"], k["brow"], k["ball"]

        @block.sync
        def _(sp):
            loads = [(k["X"][:], rows(k["x"])), (w["0"][:], k["W0"]),
                     (w["att"][:, 0:NH], k["Watt"][0:D, :]), (w["att"][:, NH:2 * NH], k["Watt"][D:2 * D, :]),
                     (w["21"][:], k["W21"]), (w["22"][:], k["W22"]), (w["31"][:], k["W31"]), (w["32"][:], k["W32"]),
                     (brow[0:1, 0, :], k["b0"]), (brow[0:1, 1, :], k["bd"]), (brow[0:1, 2, :], k["bcn"]),
                     (brow[0:1, 3, :], k["bs"]), (k["batt_row"][0:1, 0:NH], k["batt"]),
                     (ball[:, 0, :], k["b21"].partition_broadcast(P).rearrange("p a d -> p (a d)")),
                     (ball[:, 1, :], k["b22"].partition_broadcast(P).rearrange("p a d -> p (a d)")),
                     (ball[:, 2, :], k["b32"].partition_broadcast(P).rearrange("p a d -> p (a d)")),
                     (k["b31_all"][:], k["b31"].partition_broadcast(P).rearrange("p a d -> p (a d)"))]
            loads += [(raw[:, n, :], k[m]) for n, m in enumerate(("Wd", "Wc", "Ws"))]
            for to, of in loads:
                sp.dma_start(to, of).then_inc(loaded, 16)
            sp.wait_ge(loaded, 16 * len(loads))

        @block.tensor
        def _(pe):
            pe.wait_ge(loaded, 16 * 20)
            for n in range(3):
                last = nc.tensor.transpose(pt[:, n, :], raw[:, n, :], k["ident"][:])
            last.then_inc(turned, 1)

        @block.vector
        def _(dve):
            nc.vector.memset(k["batt_row"][0:1, NH:2 * NH], 0.0)
            dve.wait_ge(turned, 1)
            for n in range(3):
                nc.vector.tensor_copy(w["1"][:, n, :], pt[:, n, :])


def attention_rows(nc, k, score, row8):
    H, acc, XL, count, offset = k["H"], k["acc"], k["XL"], k["count"], k["offset"]
    one_partition = lambda t: t.rearrange("(p j) f -> p j f", p=P)
    with ExitStack() as c:
        def sb(name, shape, dt=fp32):
            return c.enter_context(nc.sbuf_tensor("at_" + name, shape, dt))

        start = sb("start", [P, 2, NT], i32)
        end = sb("end", [P, NT], i32)
        f1, f2, node = sb("f1", [P, 2, NT]), sb("f2", [P, 2, NT]), sb("node", [P, 2, NT], i32)
        gathered = sb("gathered", [P, NT, NH])
        head_key = sb("head_key", [P, 1], i32)
        head = sb("head", [P, 2 * NH])
        gate = sb("gate", [P, J])
        fl = sb("fl", [P, J])

        with ExitStack() as s:
            iota_ready, steps = s.enter_context(semaphores(nc, "iota_ready", "steps"))
            block = s.enter_context(nc.Block())

            @block.gpsimd
            def _(pool):
                nc.gpsimd.iota(node[:], [[0, 2], [P, NT]], base=EP, channel_multiplier=1).then_inc(iota_ready, 1)

            @block.vector
            def _(dve):
                v, ch = nc.vector, Count(steps)
                ch.link(dve, v.tensor_scalar(f1[:], count[:], 0.0, None, ALU.is_equal))
                dve.wait_ge(iota_ready, 1)
                ch.link(dve, v.tensor_tensor(f2[:], node[:], offset[:], ALU.subtract))
                ch.link(dve, v.tensor_tensor(f2[:], f2[:], f1[:], ALU.mult))
                ch.link(dve, v.tensor_tensor(start[:], offset[:], f2[:], ALU.add))
                ch.link(dve, v.tensor_tensor(f1[:, 0], offset[:, 1], count[:, 1], ALU.add))
                ch.link(dve, v.tensor_scalar(end[:], f1[:, 0], -1.0, 0.0, ALU.add, ALU.max))
                ch.link(dve, v.memset(acc[:], 0.0))

        def indexed(tag, jobs):
            with ExitStack() as s:
                [moved] = s.enter_context(semaphores(nc, "moved"))
                block = s.enter_context(nc.Block())

                @block.gpsimd
                def _(pool):
                    for to, to_at, of, of_at in jobs:
                        nc.gpsimd.indirect_dma_start(
                            to, bass.IndirectOffsetOnAxis(ap=to_at, axis=0) if to_at is not None else None,
                            of, bass.IndirectOffsetOnAxis(ap=of_at, axis=0) if of_at is not None else None,
                        ).then_inc(moved, 16)
                    pool.wait_ge(moved, 16 * len(jobs))

        flat = k["row_start"].rearrange("r f -> (r f)").rearrange("(p q) -> p q", p=P)
        flat4 = k["sj_start"].rearrange("r f -> (r f)").rearrange("(p q) -> p q", p=P)
        w8, w4 = (EP + NP) * 2 * NH // P, (EP + NP) * NH // P
        store(nc, (rows(k["sj_node"]), score[:, :, NH:2 * NH]), (flat4, acc[:, 0:w4]),
              (flat[:, 0:w4], acc[:, 0:w4]), (flat[:, w4:w8], acc[:, 0:w8 - w4]))
        indexed("fill_dst", [(k["sj_start"], start[:, 0, t:t + 1], score[:, t, NH:2 * NH], None) for t in range(NT)])

        with ExitStack() as d:
            ed = d.enter_context(nc.sbuf_tensor("at_edges", [P, J, 4], fp32))
            pay = d.enter_context(nc.sbuf_tensor("at_pay", [P, J, 2 * NH], fp32))
            val = acc[:, 0:J * NH].rearrange("p (j h) -> p j h", h=NH)
            sje = H[:].rearrange("p t d -> p (t d)")[:, 0:J * NH].rearrange("p (j h) -> p j h", h=NH)
            with ExitStack() as s:
                loaded, keyed, moved, steps = s.enter_context(semaphores(nc, "loaded", "keyed", "moved", "steps"))
                block = s.enter_context(nc.Block())

                @block.sync
                def _(sp):
                    sp.dma_start(ed[:], one_partition(k["edges"])).then_inc(loaded, 16)
                    sp.dma_start(val, one_partition(k["sj_start"][0:EP, :])).then_inc(loaded, 16)

                @block.gpsimd
                def _(pool):
                    pool.wait_ge(keyed, 1)
                    nc.gpsimd.indirect_dma_start(head[:, 0:NH], None, k["sj_node"],
                                                 bass.IndirectOffsetOnAxis(ap=head_key[:], axis=0)).then_inc(moved, 16)

                @block.vector
                def _(dve):
                    v, ch = nc.vector, Count(steps)
                    dve.wait_ge(loaded, 32)
                    v.tensor_copy(head_key[:], ed[:, 0, 1:2]).then_inc(keyed, 1)
                    v.memset(gate[:, 0:1], 0.0)
                    v.memset(pay[:], 0.0)
                    ch.link(dve, v.tensor_tensor(gate[:, 1:J], ed[:, 1:J, 1], ed[:, 0:J - 1, 1], ALU.is_equal))
                    dve.wait_ge(moved, 16)
                    ch.link(dve, v.tensor_copy(val[:, 0, :], head[:, 0:NH]))
                    for h in range(NH):
                        ch.link(dve, v.tensor_tensor_scan(sje[:, :, h], gate[:], val[:, :, h], 0.0, ALU.mult, ALU.add))
                    v.tensor_copy(pay[:, :, 0:NH], sje)
                    ch.link(dve, v.tensor_scalar(fl[:], ed[:, :, 2], 2.0, float(LAST), ALU.is_equal, ALU.mult))
                    ch.link(dve, v.tensor_tensor(pay[:, :, NH], fl[:], ed[:, :, 0], ALU.max))

            with ExitStack() as s:
                slot = s.enter_context(nc.sbuf_tensor("at_slot", [P, 2, U], i32))
                row = s.enter_context(nc.sbuf_tensor("at_row", [P, 2, U, 2 * NH], fp32))
                stored, staged, out0, out1, passed = s.enter_context(
                    semaphores(nc, "stored", "staged", "out0", "out1", "passed"))
                moved = (out0, out1)
                block = s.enter_context(nc.Block())

                @block.sync
                def _(sp):
                    sp.dma_start(one_partition(k["sj_edge"]), sje).then_inc(stored, 16)
                    sp.wait_ge(stored, 16)

                @block.scalar
                def _(act):
                    with act.Fori(0, STEPS) as i:
                        for g in range(2):
                            act.wait_ge(moved[g], i * (16 * U) + 16)
                            a = bass.ds(i * G2 + g * U, U)
                            nc.scalar.activation(slot[:, g], ed[:, a, 3], ACT.Copy).then_inc(staged, 1)
                            nc.scalar.activation(row[:, g], pay[:, a, :], ACT.Copy).then_inc(staged, 1)

                @block.gpsimd
                def _(pool):
                    for g in range(2):
                        pool.dma_start(k["credit"][g:g + 1, :], k["gate"][:, 0:2]).then_inc(moved[g], 16)
                    with pool.Fori(0, STEPS) as i:
                        for g in range(2):
                            pool.wait_ge(staged, i * 4 + (2 * g + 2))
                            pool.sem_inc(passed, 1)
                            for u in range(U):
                                nc.gpsimd.indirect_dma_start(
                                    k["by_src"], bass.IndirectOffsetOnAxis(ap=slot[:, g, u:u + 1], axis=0),
                                    row[:, g, u, :], None).then_inc(moved[g], 16)
                    for g in range(2):
                        pool.wait_ge(moved[g], STEPS * 16 * U + 16)

        with ExitStack() as d:
            by = d.enter_context(nc.sbuf_tensor("at_by", [P, J, 2 * NH], fp32))
            fill = d.enter_context(nc.sbuf_tensor("at_fill", [P, J, 2 * NH], fp32))
            before = d.enter_context(nc.sbuf_tensor("at_before", [P, 1], fp32))
            same = d.enter_context(nc.sbuf_tensor("at_same", [P, J], fp32))
            closed = d.enter_context(nc.sbuf_tensor("at_closed", [P, 2, NH], fp32))
            turned = d.enter_context(nc.sbuf_tensor("at_turned", [NH, 2, P], fp32))
            carry = d.enter_context(nc.sbuf_tensor("at_carry", [NH, P + 1], fp32))
            init = d.enter_context(nc.sbuf_tensor("at_init", [P, NH], fp32))
            psum = d.enter_context(nc.psum_tensor("at_ps", [P, 3, P], fp32))
            scan = acc[:, 0:J * NH].rearrange("p (j h) -> p j h", h=NH)
            val = H[:].rearrange("p t d -> p (t d)")[:, 0:J * NH].rearrange("p (j h) -> p j h", h=NH)

            def scan_over_partitions(tag, data, gates, op0, op1, none, pick, ready=None):
                with ExitStack() as s:
                    steps, ended, flipped, carried, back = s.enter_context(semaphores(nc, "steps", "ended", "flipped", "carried", "back"))
                    block = s.enter_context(nc.Block())

                    @block.tensor
                    def _(pe):
                        pe.wait_ge(ended, 1)
                        for n in range(2):
                            last = nc.tensor.transpose(psum[0:NH, n, :], closed[:, n, :], k["ident"][:])
                        last.then_inc(flipped, 1)
                        pe.wait_ge(carried, 1)
                        nc.tensor.transpose(psum[:, 2, 0:NH], carry[:, 0:P], k["ident"][0:NH, 0:NH]).then_inc(back, 1)

                    @block.vector
                    def _(dve):
                        v, ch = nc.vector, Count(steps)
                        for h in range(NH):
                            ch.link(dve, v.tensor_tensor_scan(scan[:, :, h], gates, data[:, :, h], none, op0, op1))
                        v.tensor_copy(closed[:, 0, :], scan[:, J - 1, :])
                        ch.link(dve, v.tensor_reduce(before[:], gates, AX.X, ALU.min))
                        v.tensor_copy(closed[:, 1, :], before[:].to_broadcast([P, NH])).then_inc(ended, 1)
                        ch.link(dve, v.memset(carry[:, 0:1], none))
                        dve.wait_ge(flipped, 1)
                        ch.link(dve, v.tensor_copy(turned[:], psum[0:NH, 0:2, :]))
                        v.tensor_tensor_scan(carry[:, 1:P + 1], turned[:, 1, :], turned[:, 0, :], none, op0, op1).then_inc(carried, 1)
                        dve.wait_ge(back, 1)
                        ch.link(dve, v.tensor_copy(init[:], psum[:, 2, 0:NH]))
                        for h in range(NH):
                            ch.link(dve, v.tensor_tensor_scan(scan[:, :, h], gates, data[:, :, h], init[:, h:h + 1], op0, op1))

            with ExitStack() as s:
                loaded, reset, steps = s.enter_context(semaphores(nc, "loaded", "reset", "steps"))
                block = s.enter_context(nc.Block())

                @block.sync
                def _(sp):
                    sp.dma_start(by[:], one_partition(k["by_src"])).then_inc(loaded, 16)
                    sp.wait_ge(reset, 1)
                    sp.dma_start(before[1:P, :], one_partition(k["by_src"])[0:P - 1, J - 1, NH:NH + 1],
                                 allow_slow_non_contiguous=True).then_inc(loaded, 16)

                @block.vector
                def _(dve):
                    v, ch = nc.vector, Count(steps)
                    v.memset(before[:], -1.0).then_inc(reset, 1)
                    dve.wait_ge(loaded, 32)
                    v.tensor_copy(head_key[:], by[:, 0, NH:NH + 1])
                    v.tensor_tensor(same[:, 0:1], by[:, 0, NH:NH + 1], before[:], ALU.is_equal)
                    ch.link(dve, v.tensor_tensor(same[:, 1:J], by[:, 1:J, NH], by[:, 0:J - 1, NH], ALU.is_equal))
                    ch.link(dve, v.tensor_scalar(fl[:], same[:], -1.0, BIG, ALU.add, ALU.mult))

            scan_over_partitions("max", by[:, :, 0:NH], fl[:], ALU.add, ALU.max, -BIG, None)
            store(nc, (one_partition(k["max_scan"]), scan))
            indexed("ends_max", [(gathered[:, t, :], None, k["max_scan"], end[:, t:t + 1]) for t in range(NT)])
            on_vector(nc, "max_rows",
                      lambda v: v.tensor_tensor(gathered[:], gathered[:], score[:, :, 0:NH], ALU.add),
                      lambda v: v.scalar_tensor_tensor(row8[:, :, NH:2 * NH], gathered[:], 0.2, gathered[:], ALU.mult, ALU.max),
                      lambda v: v.tensor_copy(row8[:, :, 0:NH], score[:, :, 0:NH]))
            store(nc, (rows(k["row_node"]), row8[:]))
            indexed("fill_src", [(k["row_start"], start[:, 1, t:t + 1], row8[:, t, :], None) for t in range(NT)]
                    + [(head[:], None, k["row_node"], head_key[:])])
            with ExitStack() as s:
                loaded, scored, exped, steps = s.enter_context(semaphores(nc, "loaded", "scored", "exped", "steps"))
                block = s.enter_context(nc.Block())

                @block.sync
                def _(sp):
                    sp.dma_start(fill[:], one_partition(k["row_start"][0:EP, :])).then_inc(loaded, 16)

                @block.vector
                def _(dve):
                    v, ch = nc.vector, Count(steps)
                    v.tensor_copy(gate[:], same[:])
                    ch.link(dve, v.memset(fl[:, 0:1], 0.0))
                    ch.link(dve, v.memset(gate[:, 0:1], 0.0))
                    dve.wait_ge(loaded, 16)
                    ch.link(dve, v.tensor_copy(fill[:, 0, :], head[:]))
                    for f in range(2 * NH):
                        ch.link(dve, v.tensor_tensor_scan(fill[:, :, f], gate[:], fill[:, :, f], 0.0, ALU.mult, ALU.add))
                    ch.link(dve, v.tensor_tensor(val, fill[:, :, 0:NH], by[:, :, 0:NH], ALU.add))
                    ch.link(dve, v.scalar_tensor_tensor(val, val, 0.2, val, ALU.mult, ALU.max))
                    v.tensor_tensor(val, val, fill[:, :, NH:2 * NH], ALU.subtract).then_inc(scored, 1)

                @block.scalar
                def _(act):
                    act.wait_ge(scored, 1)
                    nc.scalar.activation(val, val, ACT.Exp).then_inc(exped, 1)

            scan_over_partitions("sum", val, same[:], ALU.mult, ALU.add, 0.0, None)
            store(nc, (one_partition(k["sum_scan"]), scan))
            indexed("ends_sum", [(gathered[:, t, :], None, k["sum_scan"], end[:, t:t + 1]) for t in range(NT)])

        with ExitStack() as d:
            tab = d.enter_context(nc.sbuf_tensor("at_tab", [P, NT, AW], fp32))
            heads = lambda a: a.rearrange("p t (h c) -> p t h c", h=NH)
            on_vector(nc, "table0",
                      lambda v: v.tensor_scalar(gathered[:], gathered[:], 1e-16, None, ALU.add),
                      lambda v: v.reciprocal(gathered[:], gathered[:]),
                      *[lambda v, h=h: v.tensor_tensor(tab[:, :, h * HC:(h + 1) * HC], XL[:, :, h * HC:(h + 1) * HC],
                                                  gathered[:, :, h:h + 1].to_broadcast([P, NT, HC]), ALU.mult) for h in range(NH)],
                      lambda v: v.tensor_copy(tab[:, :, D:AW], row8[:]))
            store(nc, (rows(k["table0"]), tab[:]))


def layers(nc, k):
    X, H, acc, w, brow, ball, dinv = (k[n] for n in ("X", "H", "acc", "w", "brow", "ball", "dinv"))
    add_to = lambda to, got: nc.vector.tensor_tensor(to, to, got, ALU.add)
    wide = lambda t, n=D: t.unsqueeze(2).to_broadcast([P, NT, n])
    bias = lambda t, n=D: t.unsqueeze(1).to_broadcast([P, NT, n])

    layer_norm(nc, k, "ln0")
    with ExitStack() as s:
        XL = s.enter_context(nc.sbuf_tensor("XL", [P, NT, D], fp32))
        score = s.enter_context(nc.sbuf_tensor("score", [P, NT, 2 * NH], fp32))
        row8 = s.enter_context(nc.sbuf_tensor("row8", [P, NT, 2 * NH], fp32))
        node_loop(nc, k, "xl", H, XL, w["0"][:], brow[0:1, 0, :])
        node_loop(nc, k, "score", XL, score, w["att"][:], k["batt_row"][:], width=2 * NH)
        attention_rows(nc, k | {"XL": XL}, score, row8)
        on_vector(nc, "alone",
                  lambda v: v.tensor_tensor(XL[:], XL[:], wide(k["alone"][:]), ALU.mult),
                  lambda v: v.tensor_tensor(X[:], X[:], XL[:], ALU.add))
    with ExitStack() as s:
        sj = s.enter_context(nc.sbuf_tensor("sj_chunks", [P, J, NH], fp32))
        store(nc, (sj[:], k["sj_edge"].rearrange("(j p) f -> p j f", p=P)))
        aggregate(nc, k, "ag0", k["table0"], k["idx"], AW, D, attend=(sj, k["cap"]))
    node_loop(nc, k, "out0", acc, X, take=add_to)

    layer_norm(nc, k, "ln1")
    for n in range(3):
        with ExitStack() as s:
            made = s.enter_context(nc.sbuf_tensor(f"made1{n}", [P, NT, D], fp32))
            node_loop(nc, k, f"m1{n}", H, made, w["1"][:, n, :], brow[0:1, 1 + n, :])
            store(nc, (rows(k["table1"][n * NP:(n + 1) * NP, :]), made[:]))
    aggregate(nc, k, "ag1", k["table1"], k["idx_typed"], D, D)
    node_loop(nc, k, "out1", acc, X,
              take=lambda to, got: nc.vector.scalar_tensor_tensor(to, got, 0.0, to, ALU.max, ALU.add))

    layer_norm(nc, k, "ln2")
    for n, c in enumerate("ab"):
        on_vector(nc, "scaled2" + c, lambda v: v.tensor_tensor(H[:], H[:], wide(dinv[:]), ALU.mult))
        store(nc, (rows(k["table2"][n]), H[:]))
        aggregate(nc, k, "ag2" + c, k["table2"][n], k["idx"], D, D)
        node_loop(nc, k, "out2" + c, acc, H, w[f"2{n + 1}"][:], turn=False)
        on_vector(nc, "relu2" + c,
                  lambda v: v.tensor_tensor(H[:], H[:], wide(dinv[:]), ALU.mult),
                  lambda v: v.tensor_tensor(H[:], H[:], bias(ball[:, n, :]), ALU.add),
                  lambda v: v.tensor_scalar(H[:], H[:], 0.0, None, ALU.max))
    on_vector(nc, "x3", lambda v: v.tensor_tensor(X[:], X[:], H[:], ALU.add))

    layer_norm(nc, k, "ln3")
    with ExitStack() as s:
        narrow = s.enter_context(nc.sbuf_tensor("narrow", [P, NT, D3], fp32))
        scaled = lambda v: v.tensor_tensor(narrow[:], narrow[:], wide(dinv[:], D3), ALU.mult)
        node_loop(nc, k, "in3", H, narrow, w["31"][:], width=D3)
        on_vector(nc, "scaled3a", scaled)
        store(nc, (rows(k["table3"][0]), narrow[:]))
        aggregate(nc, k, "ag3a", k["table3"][0], k["idx"], D3, D3)
        node_loop(nc, k, "out3a", acc, narrow, width=D3)
        on_vector(nc, "mid3", scaled,
                  lambda v: v.tensor_tensor(narrow[:], narrow[:], bias(k["b31_all"][:], D3), ALU.add), scaled)
        store(nc, (rows(k["table3"][1]), narrow[:]))
        aggregate(nc, k, "ag3b", k["table3"][1], k["idx"], D3, D3)
    node_loop(nc, k, "out3b", acc, H, w["32"][:], turn=False, feat=D3)
    on_vector(nc, "x4",
              lambda v: v.tensor_tensor(H[:], H[:], wide(dinv[:]), ALU.mult),
              lambda v: v.tensor_tensor(H[:], H[:], bias(ball[:, 2, :]), ALU.add),
              lambda v: v.tensor_scalar(H[:], H[:], 0.0, None, ALU.max),
              lambda v: v.tensor_tensor(X[:], X[:], H[:], ALU.add))
    full = (N // P) * P
    store(nc, (k["out"][0:full, :].rearrange("(t p) d -> p t d", p=P), X[:, 0:N // P, :]),
          (k["out"][full:N, :], X[0:N - full, N // P, :]))


_WEIGHTS = ["L0_gnn_W_lin", "L0_gnn_b_lin", "L0_gnn_W_att", "L0_gnn_b_att", "L1_gnn_W_data", "L1_gnn_b_data",
            "L1_gnn_W_control", "L1_gnn_b_control", "L1_gnn_W_self", "L1_gnn_b_self", "L2_gnn_W1", "L2_gnn_b1",
            "L2_gnn_W2", "L2_gnn_b2", "L3_gnn_W1", "L3_gnn_b1", "L3_gnn_W2", "L3_gnn_b2"]


def kernel(**inputs):
    import numpy as _np
    import concourse.bacc as _bacc
    from concourse import mybir as _mybir
    from concourse.bass_utils import run_bass_kernel_spmd as _run

    nodes = _np.arange(N, dtype=_np.int32)
    pads = _np.full(EP - E - N, N, _np.int32)

    def columns(*parts):
        return _np.ascontiguousarray(_np.concatenate([_np.asarray(a) for a in parts]).reshape(J, P).T)

    arrays = {
        "x": _np.concatenate([_np.asarray(inputs["x"]), _np.zeros((NP - N, D), _np.float32)]),
        "e_src": columns(inputs["src"], nodes, pads),
        "e_dst": columns(inputs["dst"], nodes, pads),
        "e_type": columns(inputs["edge_type_2"], _np.full(EP - E, 2, _np.int32)),
    }
    for name in _WEIGHTS:
        a = _np.ascontiguousarray(inputs[name])
        arrays[name] = a if a.ndim == 2 else a.reshape(1, -1)
    nc = _bacc.Bacc("TRN2", target_bir_lowering=False, num_devices=1)
    args = [nc.dram_tensor(n, a.shape, _mybir.dt.from_np(a.dtype), kind="ExternalInput").ap() for n, a in arrays.items()]
    out = nc.dram_tensor("out", (N, D), _mybir.dt.float32, kind="ExternalOutput").ap()
    gnn_kernel(nc, *args, out)
    r = _run(nc, [arrays], core_ids=[0])
    return r.results[0]["out"]
```

```python
import concourse.bass as bass
from concourse import mybir
from contextlib import ExitStack, contextmanager

fp32 = mybir.dt.float32
bf16 = mybir.dt.bfloat16
i32 = mybir.dt.int32
ALU = mybir.AluOpType
ACT = mybir.ActivationFunctionType
AX = mybir.AxisListType

P = 128
N = 6250
E = 106250
D = 128
NH, HC = 4, 32
D3 = 32
NT = (N + P - 1) // P
NP = NT * P
U = 8
G2 = 2 * U
STEPS = -(-(E + N) // (P * G2))
J = STEPS * G2
EP = J * P
LAST = NP - 1
AW = D + 2 * NH
PIECES = 20
BIG = 1e30
NG = 7
LN_EPS = 1e-5


@contextmanager
def semaphores(nc, *names):
    sems = [nc.alloc_semaphore(f"{name}_{nc.next_id()}") for name in names]
    yield sems
    nc.clear_and_free_semaphores(sems)
    nc.all_engine_barrier()


class Count:

    def __init__(self, sem):
        self.sem, self.n = sem, 0

    def link(self, engine, ins):
        self.n += 1
        ins.then_inc(self.sem, 1)
        engine.wait_ge(self.sem, self.n)


def gnn_kernel(nc, x, e_src, e_dst, e_type, W0, b0, Watt, batt, Wd, bd, Wc, bcn, Ws, bs,
               W21, b21, W22, b22, W31, b31, W32, b32, out):
    ctx = ExitStack()

    credit = nc.dram_tensor("credit", (2, 2), fp32).ap()
    edges = nc.dram_tensor("edges_by_dst", (EP, 4), fp32).ap()
    sj_node = nc.dram_tensor("sj_node", (NP, NH), fp32).ap()
    sj_start = nc.dram_tensor("sj_start", (EP + NP, NH), fp32).ap()
    sj_edge = nc.dram_tensor("sj_edge", (EP, NH), fp32).ap()
    by_src = nc.dram_tensor("by_src", (EP, 2 * NH), fp32).ap()
    max_scan = nc.dram_tensor("max_scan", (EP, NH), fp32).ap()
    sum_scan = nc.dram_tensor("sum_scan", (EP, NH), fp32).ap()
    row_node = nc.dram_tensor("row_node", (NP, 2 * NH), fp32).ap()
    row_start = nc.dram_tensor("row_start", (EP + NP, 2 * NH), fp32).ap()
    table0 = nc.dram_tensor("table0", (NP, AW), fp32).ap()
    table1 = nc.dram_tensor("table1", (3 * NP, D), fp32).ap()
    table2 = [nc.dram_tensor(f"table2{c}", (NP, D), fp32).ap() for c in "ab"]
    table3 = [nc.dram_tensor(f"table3{c}", (NP, D3), fp32).ap() for c in "ab"]

    with ctx:
        def sb(name, shape, dt=fp32, c=ctx):
            return c.enter_context(nc.sbuf_tensor(name, shape, dt))

        X = sb("X", [P, NT, D])
        H = sb("H", [P, NT, D])
        acc = sb("acc", [P, NP + P])
        ident = sb("ident", [P, P])
        iota_row = sb("iota_row", [P, P])
        iota_col = sb("iota_col", [P, 1])
        ones = sb("ones", [P, P])
        above = sb("above", [P, P])
        gate = sb("gate", [1, 3])
        count = sb("count", [P, 2, NT])
        offset = sb("offset", [P, 2, NT])
        idx = sb("idx", [P, J], i32)
        idx_typed = sb("idx_typed", [P, J], i32)
        dloc = sb("dloc", [P, J])
        d0i = sb("d0i", [1, J], i32)
        cap = sb("cap", [P, J], bf16)
        dinv = sb("dinv", [P, NT])
        alone = sb("alone", [P, NT])
        w = {"0": sb("w0", [P, D]), "att": sb("watt", [P, 2 * NH]), "1": sb("w1", [P, 3, D]), "21": sb("w21", [P, D]),
             "22": sb("w22", [P, D]), "31": sb("w31", [P, D3]), "32": sb("w32", [D3, D])}
        batt_all = sb("batt_all", [P, 2 * NH])
        ball = sb("ball", [P, 7, D])
        b31_all = sb("b31_all", [P, D3])

        sort_edges(nc, locals())
        prepare_weights(nc, locals())
        layers(nc, locals())


def sort_edges(nc, k):
    ident, iota_row, iota_col, ones, above = (k[n] for n in ("ident", "iota_row", "iota_col", "ones", "above"))
    count, offset, edges = k["count"], k["offset"], k["edges"]
    with ExitStack() as c:
        def sb(name, shape, dt=fp32):
            return c.enter_context(nc.sbuf_tensor(name, shape, dt))

        raw = sb("raw", [P, 3, J], i32)
        key = sb("key", [P, 2, J], i32)
        part = sb("part", [P, 2, J], i32)
        klo = sb("klo", [P, 2, J], bf16)
        khi = sb("khi", [P, 2, J], bf16)
        iota_i = sb("iota_i", [P, P + 1], i32)
        iota_b = sb("iota_b", [P, P], bf16)
        ident_b = sb("ident_b", [P, P], bf16)
        zeros = sb("zeros", [P, P], bf16)

        with ExitStack() as s:
            loaded, iota_ready, steps = s.enter_context(semaphores(nc, "loaded", "iota_ready", "steps"))
            block = s.enter_context(nc.Block())

            @block.sync
            def _(sp):
                for n, a in enumerate((k["e_src"], k["e_dst"], k["e_type"])):
                    sp.dma_start(raw[:, n, :], a).then_inc(loaded, 16)
                sp.wait_ge(loaded, 48)

            @block.gpsimd
            def _(pool):
                nc.gpsimd.iota(iota_i[:, 0:P], [[1, P]], base=0, channel_multiplier=0).then_inc(iota_ready, 1)
                nc.gpsimd.iota(iota_i[:, P:P + 1], [[1, 1]], base=0, channel_multiplier=1).then_inc(iota_ready, 1)
                nc.gpsimd.memset(k["acc"][:], 0.0)

            @block.vector
            def _(dve):
                v, ch = nc.vector, Count(steps)
                v.memset(ones[:], 1.0)
                v.memset(zeros[:], 0.0)
                v.memset(k["gate"][:], 0.0)
                dve.wait_ge(iota_ready, 2)
                v.tensor_copy(iota_row[:], iota_i[:, 0:P])
                ch.link(dve, v.tensor_copy(iota_col[:], iota_i[:, P:P + 1]))
                v.tensor_copy(iota_b[:], iota_row[:])
                v.tensor_scalar(ident[:], iota_row[:], iota_col[:, 0:1], None, ALU.is_equal)
                v.tensor_scalar(above[:], iota_row[:], iota_col[:, 0:1], None, ALU.is_gt)
                v.tensor_scalar(ident_b[:], iota_row[:], iota_col[:, 0:1], None, ALU.is_equal)
                dve.wait_ge(loaded, 48)
                v.tensor_copy(key[:, 0, :], raw[:, 1, :])
                ch.link(dve, v.tensor_scalar(key[:, 1, :], raw[:, 2, :], 2.0, float(LAST), ALU.is_equal, ALU.mult))
                ch.link(dve, v.tensor_tensor(key[:, 1, :], key[:, 1, :], raw[:, 0, :], ALU.max))
                ch.link(dve, v.tensor_scalar(part[:], key[:], P - 1, None, ALU.bitwise_and))
                ch.link(dve, v.tensor_copy(klo[:], part[:]))
                ch.link(dve, v.tensor_scalar(part[:], key[:], 7, None, ALU.logical_shift_right))
                ch.link(dve, v.tensor_copy(khi[:], part[:]))

        def one_hots(engine, to, part, j0, op=ALU.is_equal):
            n = to.shape[3]
            return engine.tensor_tensor(
                to, iota_b[:, 0:n].unsqueeze(1).unsqueeze(1).to_broadcast([P, 2, U, n]),
                part[:, :, bass.ds(j0, U)].unsqueeze(3).to_broadcast([P, 2, U, n]), op)

        with ExitStack() as s:
            lo = s.enter_context(nc.sbuf_tensor("lo", [P, 2, 2, U, P], bf16))
            hi = s.enter_context(nc.sbuf_tensor("hi", [P, 2, 2, U, NT], bf16))
            away = s.enter_context(nc.sbuf_tensor("away", [P, 2, 2, U, NT], bf16))
            hist = [s.enter_context(nc.psum_tensor(f"hist{n}", [P, 512], fp32)) for n in range(2)]
            prefix = s.enter_context(nc.psum_tensor("prefix", [P, 2, 2, NT], fp32))
            zero_row = s.enter_context(nc.sbuf_tensor("zero_row", [P, NT], fp32))
            incl = s.enter_context(nc.sbuf_tensor("incl", [P, 2, NT], fp32))
            (moved, built, measured, absed, built_hi, used, passed, counted, copied, summed,
             steps) = s.enter_context(semaphores(
                nc, "moved", "built", "measured", "absed", "built_hi", "used", "passed", "counted", "copied", "summed", "steps"))
            block = s.enter_context(nc.Block())

            @block.sync
            def _(sp):
                w, ball = k["w"], k["ball"]
                wide = lambda b: b.partition_broadcast(P).rearrange("p a d -> p (a d)")
                flat4, flat8 = (k[n].rearrange("r f -> (r f)").rearrange("(p q) -> p q", p=P) for n in ("sj_start", "row_start"))
                w4, w8 = (EP + NP) * NH // P, (EP + NP) * 2 * NH // P
                jobs = [(k["X"][:], rows(k["x"])), (w["0"][:], k["W0"]), (w["21"][:], k["W21"]), (w["22"][:], k["W22"]),
                        (w["31"][:], k["W31"]), (w["32"][:], k["W32"]), (k["b31_all"][:], wide(k["b31"])),
                        (k["batt_all"][:, 0:NH], wide(k["batt"])), (flat4, k["acc"][:, 0:w4]),
                        (flat8[:, 0:w4], k["acc"][:, 0:w4]), (flat8[:, w4:w8], k["acc"][:, 0:w8 - w4])]
                jobs += [(ball[:, n, :], wide(k[m])) for n, m in enumerate(("b21", "b22", "b32", "b0", "bd", "bcn", "bs"))]
                for to, of in jobs:
                    sp.dma_start(to, of).then_inc(moved, 16)
                sp.wait_ge(moved, 16 * len(jobs))

            @block.vector
            def _(dve):
                v, ch = nc.vector, Count(steps)
                with dve.Fori(0, STEPS) as i:
                    for g in range(2):
                        dve.wait_ge(used, i * 2 + (g + 1))
                        one_hots(v, lo[:, g], klo, i * G2 + g * U).then_inc(built, 1)
                dve.wait_ge(counted, 1)
                for n in range(2):
                    last = v.tensor_copy(count[:, n, :], hist[n][:, 0:NT])
                last.then_inc(copied, 1)
                dve.wait_ge(summed, 1)
                for n in range(2):
                    ch.link(dve, v.tensor_tensor_scan(incl[:, n, :], prefix[:, 1, n, :], zero_row[:], 0.0, ALU.add, ALU.add))
                ch.link(dve, v.tensor_tensor(incl[:], incl[:], prefix[:, 1], ALU.subtract))
                ch.link(dve, v.tensor_tensor(offset[:], incl[:], prefix[:, 0], ALU.add))

            @block.gpsimd
            def _(pool):
                with pool.Fori(0, STEPS) as i:
                    for g in range(2):
                        pool.wait_ge(absed, i * 2 + (g + 1))
                        pool.sem_inc(passed, 1)
                        one_hots(nc.gpsimd, away[:, g], khi, i * G2 + g * U, ALU.subtract).then_inc(measured, 1)

            @block.scalar
            def _(act):
                nc.scalar.activation(zero_row[:], ones[:, 0:NT], ACT.Relu, scale=-1.0)
                act.sem_inc(absed, 2)
                with act.Fori(0, STEPS) as i:
                    for g in range(2):
                        act.wait_ge(measured, i * 2 + (g + 1))
                        act.wait_ge(used, i * 2 + (g + 1))
                        nc.scalar.activation(hi[:, g], away[:, g], ACT.Abs).then_inc(absed, 1)
                        act.wait_ge(absed, i * 2 + (g + 3))
                        nc.scalar.activation(hi[:, g], hi[:, g], ACT.Relu, bias=ones[:, 0:1], scale=-1.0).then_inc(built_hi, 1)

            @block.tensor
            def _(pe):
                for n in range(2):
                    last = nc.tensor.matmul(hist[n][:, 0:NT], zeros[:], zeros[:, 0:NT], start=True, stop=False)
                last.then_inc(used, 2)
                with pe.Fori(0, STEPS) as i:
                    for g in range(2):
                        pe.wait_ge(built, i * 2 + (g + 1))
                        pe.wait_ge(built_hi, i * 2 + (g + 1))
                        for n in range(2):
                            for u in range(U):
                                last = nc.tensor.matmul(hist[n][:, 0:NT], lo[:, g, n, u, :], hi[:, g, n, u, :],
                                                        start=False, stop=False)
                        last.then_inc(used, 1)
                for n in range(2):
                    last = nc.tensor.matmul(hist[n][:, 0:NT], zeros[:], zeros[:, 0:NT], start=False, stop=True)
                last.then_inc(counted, 1)
                pe.wait_ge(copied, 1)
                for n in range(2):
                    nc.tensor.matmul(prefix[:, 0, n, :], above[:], count[:, n, :], start=True, stop=True)
                    last = nc.tensor.matmul(prefix[:, 1, n, :], ones[:], count[:, n, :], start=True, stop=True)
                last.then_inc(summed, 1)

        with ExitStack() as s:
            def tb(name, shape, dt=fp32):
                return s.enter_context(nc.sbuf_tensor("place_" + name, shape, dt))

            lo = tb("lo", [P, 2, 2, U, P], bf16)
            hi = tb("hi", [P, 2, 2, U, NT], bf16)
            loT = tb("loT", [P, 2, 2, U, P])
            same = tb("same", [P, 2, 2, U, P], bf16)
            base = tb("base", [P, 2, 2, U, NT])
            away = tb("away", [P, 2, U, NT], bf16)
            khi_neg = tb("khi_neg", [P, 2, J])
            picked = tb("picked", [P, 2, U, NT])
            placef = tb("placef", [P, 2, U])
            place = tb("place", [P, 2, U], i32)
            row = tb("row", [P, 2, U, 4])
            penalty = tb("penalty", [P, P], bf16)
            flipped = [s.enter_context(nc.psum_tensor(f"flipped{n}", [P, U, P], bf16)) for n in range(2)]
            masked = s.enter_context(nc.psum_tensor("masked", [P, U, P], fp32))
            cum = [s.enter_context(nc.psum_tensor(f"cum{n}", [P, U, 64], fp32)) for n in range(2)]
            look = [s.enter_context(nc.psum_tensor(f"look{n}", [P, U, 64], fp32)) for n in range(2)]
            (spread, barred, absed, high, turned, matched, hot, cummed, stepped, based, looked, weighed, placed, rowed,
             scat0, scat1, passed, ready, summed) = s.enter_context(semaphores(
                 nc, "spread", "barred", "absed", "high", "turned", "matched", "hot", "cummed", "stepped", "based",
                 "looked", "weighed", "placed", "rowed", "scat0", "scat1", "passed", "ready", "summed"))
            scattered = (scat0, scat1)
            block = s.enter_context(nc.Block())

            def over_groups(engine, before, main):
                before(0, 0)
                with engine.Fori(0, STEPS - 1) as i:
                    for g in range(2):
                        main(i, g, (i, 1) if g == 0 else (i + 1, 0))
                main(STEPS - 1, 0, (STEPS - 1, 1))
                main(STEPS - 1, 1, None)

            @block.scalar
            def _(act):
                def turn(i, g):
                    for n in range(2):
                        m = i * 4 + (2 * g + n)
                        act.wait_ge(spread, m + 1)
                        act.wait_ge(looked, m + 1)
                        nc.scalar.activation(loT[:, g, n], flipped[n][:], ACT.Copy).then_inc(turned, 1)

                def high_parts(i, g):
                    for n in range(2):
                        for u in range(U):
                            last = nc.scalar.activation(away[:, n, u, :], iota_b[:, 0:NT], ACT.Abs,
                                                        bias=khi_neg[:, n, bass.ds(i * G2 + (g * U + u), 1)])
                    last.then_inc(absed, 1)
                    act.wait_ge(absed, i * 2 + (g + 1))
                    nc.scalar.activation(hi[:, g], away[:], ACT.Relu, bias=k["ones"][:, 0:1], scale=-1.0).then_inc(high, 1)

                def before(i, g):
                    high_parts(i, g)
                    turn(i, g)

                def main(i, g, ahead):
                    if ahead is not None:
                        act.wait_ge(weighed, i * 4 + (2 * g + 2))
                        high_parts(*ahead)
                    act.wait_ge(scattered[g], i * (16 * U) + 16)
                    nc.scalar.activation(row[:, g, :, 0:3], raw[:, :, bass.ds(i * G2 + g * U, U)].rearrange("p f u -> p u f"),
                                         ACT.Copy).then_inc(rowed, 1)
                    act.wait_ge(summed, i * 4 + (2 * g + 1))
                    nc.scalar.activation(place[:, g], placef[:, g], ACT.Copy).then_inc(placed, 1)
                    if ahead is not None:
                        turn(*ahead)

                act.sem_inc(turned, 2)
                act.wait_ge(ready, 1)
                over_groups(act, before, main)

            @block.tensor
            def _(pe):
                def spread_out(i, g, n):
                    m = i * 4 + (2 * g + n)
                    pe.wait_ge(matched, m + 1)
                    for v0 in range(0, U, 4):
                        nc.tensor.matmul(masked[:, v0:v0 + 4, :], ident_b[:], penalty[:].unsqueeze(1).to_broadcast([P, 4, P]),
                                         start=True, stop=False)
                        for u in range(v0, v0 + 4):
                            low = klo[:, n, bass.ds(i * G2 + (g * U + u), 1)].to_broadcast([P, P])
                            last = nc.tensor.matmul(masked[:, u, :], low, ident_b[:], start=False, stop=u == v0 + 3)
                    last.then_inc(barred, 1)

                def turn(i, g, n):
                    m = i * 4 + (2 * g + n)
                    pe.wait_ge(hot, i * 2 + (g + 1))
                    pe.wait_ge(turned, m + 1)
                    for u in range(U):
                        last = nc.tensor.transpose(flipped[n][:, u, :], lo[:, g, n, u, :], ident_b[:])
                    last.then_inc(spread, 1)

                def add_up(i, g, n):
                    m = i * 4 + (2 * g + n)
                    pe.wait_ge(hot, i * 2 + (g + 1))
                    pe.wait_ge(high, i * 2 + (g + 1))
                    pe.wait_ge(based, m + 1)
                    for v0 in range(0, U, 4):
                        for u in range(v0, v0 + 4):
                            for w in range(v0, u + 1):
                                last = nc.tensor.matmul(cum[n][:, u, 0:NT], lo[:, g, n, w, :], hi[:, g, n, w, :],
                                                        start=w == v0, stop=w == u)
                    last.then_inc(cummed, 1)

                def look_up(i, g, n):
                    m = i * 4 + (2 * g + n)
                    pe.wait_ge(based, m + 3)
                    pe.wait_ge(turned, m + 3)
                    pe.wait_ge(weighed, m + 1)
                    for u in range(U):
                        nc.tensor.matmul(look[n][:, u, 0:NT], loT[:, g, n, u, :],
                                         base[:, g, n, u - 1, :] if u else base[:, 1 - g, n, U - 1, :], start=True, stop=False)
                        last = nc.tensor.matmul(look[n][:, u, 0:NT], same[:, g, n, u, :], hi[:, g, n, u, :], start=False, stop=True)
                    last.then_inc(looked, 1)

                def before(i, g):
                    for n in range(2):
                        spread_out(i, g, n)
                    count_and_turn(i, g)

                def count_and_turn(i, g):
                    for n in range(2):
                        add_up(i, g, n)
                    for n in range(2):
                        turn(i, g, n)

                def main(i, g, ahead):
                    for n in range(2):
                        if ahead is not None:
                            spread_out(*ahead, n)
                        look_up(i, g, n)
                    if ahead is not None:
                        count_and_turn(*ahead)

                pe.sem_inc(looked, 4)
                pe.wait_ge(ready, 1)
                over_groups(pe, before, main)

            @block.vector
            def _(dve):
                v = nc.vector

                def before(i, g):
                    j0 = i * G2 + g * U
                    dve.wait_ge(looked, i * 4 + (2 * g + 2))
                    for n in range(2):
                        if n == 1:
                            one_hots(v, lo[:, g], klo, j0).then_inc(hot, 1)
                        dve.wait_ge(barred, i * 4 + (2 * g + n + 1))
                        v.tensor_tensor(same[:, g, n], masked[:], klo[:, n, bass.ds(j0, U)].unsqueeze(2).to_broadcast([P, U, P]),
                                        ALU.is_equal).then_inc(matched, 1)

                def main(i, g, ahead):
                    for n in range(2):
                        m = i * 4 + (2 * g + n)
                        dve.wait_ge(cummed, m + 1)
                        dve.wait_ge(based, m + 1)
                        v.tensor_tensor(base[:, g, n, 0:4, :], cum[n][:, 0:4, 0:NT],
                                        base[:, 1 - g, n, U - 1:U, :].to_broadcast([P, 4, NT]), ALU.add).then_inc(stepped, 1)
                    for n in range(2):
                        m = i * 4 + (2 * g + n)
                        dve.wait_ge(stepped, m + 1)
                        v.tensor_tensor(base[:, g, n, 4:8, :], cum[n][:, 4:8, 0:NT],
                                        base[:, g, n, 3:4, :].to_broadcast([P, 4, NT]), ALU.add).then_inc(based, 1)
                    if ahead is not None:
                        before(*ahead)
                    for n in range(2):
                        m = i * 4 + (2 * g + n)
                        dve.wait_ge(looked, m + 5)
                        v.tensor_tensor(picked[:, n], look[n][:, :, 0:NT], hi[:, g, n], ALU.mult).then_inc(weighed, 1)
                        dve.wait_ge(weighed, m + 3)
                        dve.wait_ge(scattered[g], i * (16 * U) + 16)
                        v.tensor_reduce(placef[:, g] if n == 0 else row[:, g, :, 3], picked[:, n], AX.X,
                                        ALU.add).then_inc(summed, 1)

                v.tensor_copy(base[:, 1, :, U - 1, :], offset[:]).then_inc(based, 2)
                v.tensor_scalar(khi_neg[:], khi[:], -1.0, None, ALU.mult)
                v.tensor_scalar(penalty[:], above[:], -512.0, 512.0, ALU.mult, ALU.add).then_inc(ready, 1)
                dve.sem_inc(matched, 1)
                dve.sem_inc(weighed, 2)
                over_groups(dve, before, main)

            @block.gpsimd
            def _(pool):
                for g in range(2):
                    pool.dma_start(k["credit"][g:g + 1, :], k["gate"][:, 0:2]).then_inc(scattered[g], 16)
                with pool.Fori(0, STEPS) as i:
                    for g in range(2):
                        pool.wait_ge(rowed, i * 2 + (g + 1))
                        pool.wait_ge(placed, i * 2 + (g + 1))
                        pool.wait_ge(summed, i * 4 + (2 * g + 2))
                        pool.sem_inc(passed, 1)
                        for u in range(U):
                            nc.gpsimd.indirect_dma_start(
                                edges, bass.IndirectOffsetOnAxis(ap=place[:, g, u:u + 1], axis=0),
                                row[:, g, u, :], None).then_inc(scattered[g], 16)
                for g in range(2):
                    pool.wait_ge(scattered[g], STEPS * 16 * U + 16)


def node_stage(nc, k, tag, feat=0, weight=None, land=(), norm=False, products=(), after=None, store=None):
    X, acc, ident = k["X"], k["acc"], k["ident"]
    NS = NT // NG
    n_ahead = len(land) + (5 if norm else 0)
    n_made = len(products)
    at = lambda i: bass.ds(i * NG, NG)
    nothing = lambda i: None
    with ExitStack() as s:
        def tb(name, shape):
            return s.enter_context(nc.sbuf_tensor(f"{tag}_{name}", shape, fp32))

        tiles = tb("tiles", [P, NG, P]) if feat else None
        moments = tb("moments", [P, NG, 6]) if norm else None
        mean_var = tb("mean_var", [P, NG, 2]) if norm else None
        scale = tb("scale", [P, NG]) if norm else None
        shift = tb("shift", [P, NG]) if norm else None
        normed = tb("normed", [P, NG, D]) if products else None
        turned = tb("turned", [P, NG, P]) if products else None
        p_in = s.enter_context(nc.psum_tensor(tag + "_p_in", [P, NG + 1, P], fp32))
        p_turn = s.enter_context(nc.psum_tensor(tag + "_p_turn", [P, NG + 1, P], fp32))
        p_made = s.enter_context(nc.psum_tensor(tag + "_p_made", [P, 2, NG + 1, P], fp32))
        staged, fed, ahead, rooted, normal, flipped, kept, made, taken, done, passed, stored = s.enter_context(semaphores(
            nc, "staged", "fed", "ahead", "rooted", "normal", "flipped", "kept", "made", "taken", "done", "passed", "stored"))
        block = s.enter_context(nc.Block())

        def over_steps(engine, first, rest):
            for part in first:
                part(0)
            with engine.Fori(0, NS - 1) as i:
                for n in range(max(len(first), len(rest))):
                    for part in rest[n:n + 1]:
                        part(i)
                    for part in first[n:n + 1]:
                        part(i + 1)
            for part in rest:
                part(NS - 1)

        def columns(i):
            return tiles[0:feat].rearrange("p t d -> p (t d)"), acc[0:feat, bass.ds(i * (NG * P), NG * P)]

        if feat and norm:
            @block.gpsimd
            def _(pool):
                with pool.Fori(0, NS) as i:
                    pool.wait_ge(fed, i + 1)
                    pool.sem_inc(passed, 1)
                    nc.gpsimd.tensor_copy(*columns(i)).then_inc(staged, 1)

        @block.scalar
        def _(act):
            def stage(i):
                if feat and not norm:
                    act.wait_ge(fed, i + 1)
                    nc.scalar.activation(*columns(i), ACT.Copy).then_inc(staged, 1)

            def root(i):
                if norm:
                    act.wait_ge(ahead, i * n_ahead + (2 * n_ahead - 2))
                    nc.scalar.activation(scale[:], scale[:], ACT.Sqrt).then_inc(rooted, 1)

            def normalise(i):
                if norm:
                    act.wait_ge(ahead, i * n_ahead + 2 * n_ahead)
                    if products:
                        act.wait_ge(flipped, i + 1)
                    for u in range(NG):
                        to = normed[:, u, :] if products else \
                            k["H"][:, bass.ds(i * NG + u, 1), :].rearrange("p t d -> p (t d)")
                        last = nc.scalar.activation(to, X[:, bass.ds(i * NG + u, 1), :].rearrange("p t d -> p (t d)"),
                                                    ACT.Relu, bias=shift[:, u:u + 1], scale=scale[:, u:u + 1])
                    last.then_inc(normal, 1)

            def turn(i):
                if products:
                    act.wait_ge(flipped, i + 2)
                    act.wait_ge(made, i * n_made + n_made)
                    nc.scalar.activation(turned[:], p_turn[:, 0:NG, :], ACT.Copy).then_inc(kept, 1)

            act.sem_inc(normal, 1)
            act.sem_inc(kept, 1)
            over_steps(act, [stage, root, normalise], [turn])

        @block.tensor
        def _(pe):
            def feed(i):
                if feat:
                    pe.wait_ge(staged, i + 1)
                    pe.wait_ge(ahead, i * n_ahead + n_ahead)
                    pe.sem_inc(passed, 1)
                    for u in range(NG):
                        if weight is None:
                            last = nc.tensor.transpose(p_in[:, u, 0:feat], tiles[0:feat, u, :], ident[0:feat, 0:feat])
                        else:
                            last = nc.tensor.matmul(p_in[:, u, :], tiles[0:feat, u, :], weight, start=True, stop=True)
                    last.then_inc(fed, 1)

            def flip(i):
                if not products:
                    return
                pe.wait_ge(normal, i + 2)
                pe.wait_ge(kept, i + 1)
                for u in range(NG):
                    last = nc.tensor.transpose(p_turn[:, u, :], normed[:, u, :], ident[:])
                last.then_inc(flipped, 1)

            def make(i):
                for n, (w, width, _) in enumerate(products):
                    pe.wait_ge(kept, i + 2)
                    pe.wait_ge(taken, i * n_made + (n_made + max(n - 1, 0)))
                    for u in range(NG):
                        last = nc.tensor.matmul(p_made[:, n % 2, u, 0:width], turned[:, u, :], w, start=True, stop=True)
                    last.then_inc(made, 1)

            pe.sem_inc(fed, 1)
            pe.sem_inc(flipped, 1)
            if products:
                pe.sem_inc(made, n_made)
            over_steps(pe, [feed], [nothing, flip, make])

        @block.vector
        def _(dve):
            v = nc.vector

            def ready(i):
                c = 0
                if feat:
                    dve.wait_ge(fed, i + 2)
                for op in land:
                    op(v, at(i), p_in[:, 0:NG, 0:feat if weight is None else D]).then_inc(ahead, 1)
                    c += 1
                    dve.wait_ge(ahead, i * n_ahead + (n_ahead + c))
                if not norm:
                    return
                dve.sem_inc(passed, 1)
                for u in range(NG):
                    last = v.bn_stats(moments[:, u, :], X[:, bass.ds(i * NG + u, 1), :].rearrange("p t d -> p (t d)"))
                last.then_inc(ahead, 1)
                dve.wait_ge(ahead, i * n_ahead + (n_ahead + c + 1))
                dve.sem_inc(passed, 1)
                for u in range(NG):
                    last = v.bn_aggr(mean_var[:, u, :], moments[:, u, :])
                last.then_inc(ahead, 1)
                dve.wait_ge(ahead, i * n_ahead + (n_ahead + c + 2))
                dve.wait_ge(normal, i + 1)
                v.tensor_scalar(scale[:], mean_var[:, :, 1], LN_EPS, None, ALU.add).then_inc(ahead, 1)

            def scales(i):
                if norm:
                    dve.wait_ge(rooted, i + 1)
                    v.reciprocal(scale[:], scale[:]).then_inc(ahead, 1)
                    dve.wait_ge(ahead, i * n_ahead + (2 * n_ahead - 1))
                    v.scalar_tensor_tensor(shift[:], mean_var[:, :, 0], -1.0, scale[:], ALU.mult, ALU.mult).then_inc(ahead, 1)

            def take(i):
                for n, (_, width, op) in enumerate(products):
                    dve.wait_ge(made, i * n_made + (n_made + n + 1))
                    op(v, at(i), p_made[:, n % 2, 0:NG, 0:width]).then_inc(taken, 1)
                if after is not None:
                    dve.wait_ge(normal, i + 2)
                    after(v, at(i)).then_inc(done, 1)

            dve.sem_inc(ahead, n_ahead)
            if n_made:
                dve.sem_inc(taken, n_made)
            over_steps(dve, [ready, scales], [nothing, nothing, take])

        if store is not None:
            @block.sync
            def _(sp):
                def wait(i):
                    if n_made:
                        sp.wait_ge(taken, i * n_made + 2 * n_made)
                    elif after is not None:
                        sp.wait_ge(done, i + 1)
                    else:
                        sp.wait_ge(ahead, i * n_ahead + 2 * n_ahead)

                n = 0
                with sp.Fori(0, NS - 1) as i:
                    wait(i)
                    for transfer in store(sp, at(i), False):
                        transfer.then_inc(stored, 16)
                        n += NS - 1
                wait(NS - 1)
                for transfer in store(sp, slice((NS - 1) * NG, NT), True):
                    transfer.then_inc(stored, 16)
                    n += 1
                sp.wait_ge(stored, 16 * n)


def on_vector(nc, *ops):
    with ExitStack() as s:
        [steps] = s.enter_context(semaphores(nc, "steps"))
        block = s.enter_context(nc.Block())

        @block.vector
        def _(dve):
            ch = Count(steps)
            for op in ops:
                ch.link(dve, op(nc.vector))


def store(nc, *pairs):
    with ExitStack() as s:
        [stored] = s.enter_context(semaphores(nc, "stored"))
        block = s.enter_context(nc.Block())

        @block.sync
        def _(sp):
            for to, of in pairs:
                sp.dma_start(to, of).then_inc(stored, 16)
            sp.wait_ge(stored, 16 * len(pairs))


def rows(table):
    return table.rearrange("(t p) f -> p t f", p=P)


def aggregate(nc, k, tag, table, idx, width, feat, attend=None):
    acc, dloc, d0i = k["acc"], k["dloc"], k["d0i"]
    with ExitStack() as s:
        def tb(name, shape, dt=fp32):
            return s.enter_context(nc.sbuf_tensor(f"{tag}_{name}", shape, dt))

        got = tb("got", [P, 2, U, width])
        slot = tb("slot", [P, 2, U], i32)
        sel = tb("sel", [P, 2, U, P])
        if attend is not None:
            msg = tb("msg", [P, 2, U, D])
            z = tb("z", [P, 2, U, NH])
            sj, cap = attend
        part = s.enter_context(nc.psum_tensor(f"{tag}_part", [P, 2, U, P], fp32))
        names = ("got0", "got1", "slotted", "selected", "summed", "added", "scored", "exped", "ready", "passed")
        got0, got1, slotted, selected, summed, added, scored, exped, ready, passed = s.enter_context(semaphores(nc, *names))
        arrived = (got0, got1)
        used = summed if attend is None else ready
        block = s.enter_context(nc.Block())

        @block.scalar
        def _(act):
            def stage(i, g):
                act.wait_ge(used, i * 2 + (g + 1))
                nc.scalar.activation(slot[:, g], idx[:, bass.ds(i * G2 + g * U, U)], ACT.Copy).then_inc(slotted, 1)

            def exp(i, g):
                if attend is not None:
                    act.wait_ge(scored, i * 8 + (4 * g + 4))
                    nc.scalar.activation(z[:, g], z[:, g], ACT.Exp).then_inc(exped, 1)

            stage(0, 0)
            with act.Fori(0, STEPS - 1) as i:
                stage(i, 1)
                exp(i, 0)
                stage(i + 1, 0)
                exp(i, 1)
            stage(STEPS - 1, 1)
            exp(STEPS - 1, 0)
            exp(STEPS - 1, 1)

        @block.gpsimd
        def _(pool):
            with pool.Fori(0, STEPS) as i:
                for g in range(2):
                    pool.wait_ge(used, i * 2 + (g + 1))
                    pool.wait_ge(slotted, i * 2 + (g + 1))
                    pool.sem_inc(passed, 1)
                    for u in range(U):
                        nc.gpsimd.indirect_dma_start(
                            got[:, g, u, :], None, table,
                            bass.IndirectOffsetOnAxis(ap=slot[:, g, u:u + 1], axis=0)).then_inc(arrived[g], 16)

        @block.tensor
        def _(pe):
            pe.sem_inc(summed, 2)
            with pe.Fori(0, STEPS) as i:
                for g in range(2):
                    pe.wait_ge(selected, i * 2 + (g + 1))
                    if attend is None:
                        pe.wait_ge(arrived[g], i * (16 * U) + 16 * U)
                    else:
                        pe.wait_ge(ready, i * 2 + (g + 3))
                    pe.wait_ge(added, i * (2 * U) + (g * U + U))
                    rows_of = got if attend is None else msg
                    for u in range(U):
                        last = nc.tensor.matmul(part[0:feat, g, u, :], rows_of[:, g, u, 0:feat], sel[:, g, u, :],
                                                start=True, stop=True)
                    last.then_inc(summed, 1)

        @block.vector
        def _(dve):
            v = nc.vector

            def front(i, g):
                j0 = i * G2 + g * U
                dve.wait_ge(summed, i * 2 + (g + 1))
                v.tensor_tensor(sel[:, g], k["iota_row"][:].unsqueeze(1).to_broadcast([P, U, P]),
                                dloc[:, bass.ds(j0, U)].unsqueeze(2).to_broadcast([P, U, P]), ALU.is_equal).then_inc(selected, 1)
                if attend is None:
                    return
                dve.wait_ge(arrived[g], i * (16 * U) + 16 * U)
                n = i * 8 + 4 * g
                v.tensor_tensor(z[:, g], got[:, g, :, D:D + NH], sj[:, bass.ds(j0, U), :], ALU.add).then_inc(scored, 1)
                dve.wait_ge(scored, n + 1)
                v.scalar_tensor_tensor(z[:, g], z[:, g], 0.2, z[:, g], ALU.mult, ALU.max).then_inc(scored, 1)
                dve.wait_ge(scored, n + 2)
                v.tensor_tensor(z[:, g], z[:, g], got[:, g, :, D + NH:D + 2 * NH], ALU.subtract).then_inc(scored, 1)
                dve.wait_ge(scored, n + 3)
                v.tensor_tensor(z[:, g], z[:, g], cap[:, bass.ds(j0, U)].unsqueeze(2).to_broadcast([P, U, NH]),
                                ALU.min).then_inc(scored, 1)
                dve.wait_ge(exped, i * 2 + (g + 1))
                v.tensor_tensor(msg[:, g].rearrange("p u (h c) -> p u h c", h=NH),
                                got[:, g, :, 0:D].rearrange("p u (h c) -> p u h c", h=NH),
                                z[:, g].unsqueeze(3).to_broadcast([P, U, NH, HC]), ALU.mult).then_inc(ready, 1)

            def add(i, g):
                _, at = nc.values_load_multi_w_load_instructions(
                    d0i[0:1, bass.ds(i * G2 + g * U, U)], engines=[mybir.EngineType.DVE], min_val=0, max_val=NP,
                    skip_runtime_bounds_check_because="destinations are nodes")
                dve.wait_ge(summed, i * 2 + (g + 3))
                for u in range(U):
                    dve.wait_ge(added, i * (2 * U) + (g * U + 2 * U + u))
                    w = acc[0:feat, bass.ds(at[u], P)]
                    v.tensor_tensor(w, w, part[0:feat, g, u, :], ALU.add).then_inc(added, 1)

            v.memset(acc[:], 0.0).then_inc(added, 2 * U)
            if attend is not None:
                dve.sem_inc(ready, 2)
            front(0, 0)
            with dve.Fori(0, STEPS - 1) as i:
                front(i, 1)
                add(i, 0)
                front(i + 1, 0)
                add(i, 1)
            front(STEPS - 1, 1)
            add(STEPS - 1, 0)
            add(STEPS - 1, 1)


def prepare_weights(nc, k):
    with ExitStack() as s:
        raw = s.enter_context(nc.sbuf_tensor("raw_w", [P, 4, D], fp32))
        b0_wide = s.enter_context(nc.sbuf_tensor("b0_wide", [P, P], fp32))
        b0_col = s.enter_context(nc.sbuf_tensor("b0_col", [P, 1], fp32))
        w0T = s.enter_context(nc.sbuf_tensor("w0T", [P, D], fp32))
        att = s.enter_context(nc.sbuf_tensor("raw_att", [P, 2 * NH], fp32))
        pt = s.enter_context(nc.psum_tensor("turned_w", [P, 4, P], fp32))
        pa = s.enter_context(nc.psum_tensor("att_w", [P, 2, 2 * NH], fp32))
        loaded, turned, kept, fused = s.enter_context(semaphores(nc, "loaded", "turned", "kept", "fused"))
        block = s.enter_context(nc.Block())
        w = k["w"]
        loads = [(att[:, 0:NH], k["Watt"][0:D, :]), (att[:, NH:2 * NH], k["Watt"][D:2 * D, :]),
                 (b0_col[:], k["b0"].rearrange("a d -> d a"))]
        loads += [(raw[:, n, :], k[m]) for n, m in enumerate(("Wd", "Wc", "Ws", "W0"))]

        @block.sync
        def _(sp):
            for to, of in loads:
                sp.dma_start(to, of, allow_slow_non_contiguous=True).then_inc(loaded, 16)
            sp.wait_ge(loaded, 16 * len(loads))

        @block.tensor
        def _(pe):
            pe.wait_ge(loaded, 16 * len(loads))
            for n in range(4):
                last = nc.tensor.transpose(pt[:, n, :], raw[:, n, :], k["ident"][:])
            last.then_inc(turned, 1)
            pe.wait_ge(kept, 1)
            nc.tensor.matmul(pa[:, 0, :], w0T[:], att[:], start=True, stop=True)
            nc.tensor.matmul(pa[:, 1, :], b0_wide[:], att[:], start=True, stop=True).then_inc(fused, 1)

        @block.vector
        def _(dve):
            nc.vector.memset(k["batt_all"][:, NH:2 * NH], 0.0)
            dve.wait_ge(loaded, 16 * len(loads))
            nc.vector.tensor_copy(b0_wide[:], b0_col[:].to_broadcast([P, P]))
            dve.wait_ge(turned, 1)
            nc.vector.tensor_copy(w0T[:], pt[:, 3, :]).then_inc(kept, 1)
            for n in range(3):
                nc.vector.tensor_copy(w["1"][:, n, :], pt[:, n, :])
            dve.wait_ge(fused, 1)
            nc.vector.tensor_copy(w["att"][:], pa[:, 0, :])
            nc.vector.tensor_tensor(k["batt_all"][:], k["batt_all"][:], pa[:, 1, :], ALU.add)


def attention_rows(nc, k, score, row8, sj):
    H, acc, XL, count, offset = k["H"], k["acc"], k["XL"], k["count"], k["offset"]
    one_partition = lambda t: t.rearrange("(p j) f -> p j f", p=P)
    with ExitStack() as c:
        def sb(name, shape, dt=fp32):
            return c.enter_context(nc.sbuf_tensor("at_" + name, shape, dt))

        start = sb("start", [P, 2, NT], i32)
        end = sb("end", [P, NT], i32)
        f1, f2, node = sb("f1", [P, 2, NT]), sb("f2", [P, 2, NT]), sb("node", [P, 2, NT], i32)
        gathered = sb("gathered", [P, NT, NH])
        head_key = sb("head_key", [P, 1], i32)
        head = sb("head", [P, 2 * NH])
        gate = sb("gate", [P, J])

        with ExitStack() as s:
            iota_ready, steps = s.enter_context(semaphores(nc, "iota_ready", "steps"))
            block = s.enter_context(nc.Block())

            @block.gpsimd
            def _(pool):
                nc.gpsimd.iota(node[:], [[0, 2], [P, NT]], base=EP, channel_multiplier=1).then_inc(iota_ready, 1)

            @block.vector
            def _(dve):
                v, ch = nc.vector, Count(steps)
                ch.link(dve, v.tensor_scalar(f1[:], count[:], 0.0, None, ALU.is_equal))
                dve.wait_ge(iota_ready, 1)
                ch.link(dve, v.tensor_tensor(f2[:], node[:], offset[:], ALU.subtract))
                ch.link(dve, v.tensor_tensor(f2[:], f2[:], f1[:], ALU.mult))
                ch.link(dve, v.tensor_tensor(start[:], offset[:], f2[:], ALU.add))
                ch.link(dve, v.tensor_tensor(f1[:, 0], offset[:, 1], count[:, 1], ALU.add))
                ch.link(dve, v.tensor_scalar(end[:], f1[:, 0], -1.0, 0.0, ALU.add, ALU.max))

        def indexed(jobs):
            with ExitStack() as s:
                [moved] = s.enter_context(semaphores(nc, "moved"))
                block = s.enter_context(nc.Block())

                @block.gpsimd
                def _(pool):
                    for to, to_at, of, of_at in jobs:
                        nc.gpsimd.indirect_dma_start(
                            to, bass.IndirectOffsetOnAxis(ap=to_at, axis=0) if to_at is not None else None,
                            of, bass.IndirectOffsetOnAxis(ap=of_at, axis=0) if of_at is not None else None,
                        ).then_inc(moved, 16)
                    pool.wait_ge(moved, 16 * len(jobs))

        store(nc, (rows(k["sj_node"]), score[:, :, NH:2 * NH]))
        indexed([(k["sj_start"], start[:, 0, t:t + 1], score[:, t, NH:2 * NH], None) for t in range(NT)])

        with ExitStack() as d:
            ed = d.enter_context(nc.sbuf_tensor("at_edges", [P, J, 4], fp32))
            row = d.enter_context(nc.sbuf_tensor("at_row", [P, 2, U, 2 * NH], fp32))
            pay = d.enter_context(nc.sbuf_tensor("at_pay", [P, J, NH + 1], fp32))
            val = acc[:, 0:J * NH].rearrange("p (j h) -> p j h", h=NH)
            sje = H[:].rearrange("p t d -> p (t d)")[:, 0:J * NH].rearrange("p (j h) -> p j h", h=NH)
            with ExitStack() as s:
                loaded, keyed, moved, steps = s.enter_context(semaphores(nc, "loaded", "keyed", "moved", "steps"))
                block = s.enter_context(nc.Block())

                @block.sync
                def _(sp):
                    sp.dma_start(ed[:], one_partition(k["edges"])).then_inc(loaded, 16)
                    sp.dma_start(val, one_partition(k["sj_start"][0:EP, :])).then_inc(loaded, 16)

                @block.gpsimd
                def _(pool):
                    pool.wait_ge(keyed, 1)
                    nc.gpsimd.indirect_dma_start(head[:, 0:NH], None, k["sj_node"],
                                                 bass.IndirectOffsetOnAxis(ap=head_key[:], axis=0)).then_inc(moved, 16)

                @block.vector
                def _(dve):
                    v, ch = nc.vector, Count(steps)
                    dve.wait_ge(loaded, 32)
                    v.tensor_copy(head_key[:], ed[:, 0, 1:2]).then_inc(keyed, 1)
                    v.memset(gate[:, 0:1], 0.0)
                    v.memset(row[:], 0.0)
                    ch.link(dve, v.tensor_tensor(gate[:, 1:J], ed[:, 1:J, 1], ed[:, 0:J - 1, 1], ALU.is_equal))
                    dve.wait_ge(moved, 16)
                    ch.link(dve, v.tensor_copy(val[:, 0, :], head[:, 0:NH]))
                    for h in range(NH):
                        ch.link(dve, v.tensor_tensor_scan(sje[:, :, h], gate[:], val[:, :, h], 0.0, ALU.mult, ALU.add))
                    v.tensor_copy(pay[:, :, 0:NH], sje)
                    ch.link(dve, v.tensor_scalar(gate[:], ed[:, :, 2], 2.0, float(LAST), ALU.is_equal, ALU.mult))
                    ch.link(dve, v.tensor_tensor(pay[:, :, NH], gate[:], ed[:, :, 0], ALU.max))

            with ExitStack() as s:
                slot = s.enter_context(nc.sbuf_tensor("at_slot", [P, 2, U], i32))
                es = s.enter_context(nc.sbuf_tensor("sorted_chunks", [P, J, 4], fp32))
                d0 = s.enter_context(nc.sbuf_tensor("first_dst", [1, J], fp32))
                root = s.enter_context(nc.sbuf_tensor("root", [P, NT], fp32))
                first = s.enter_context(nc.psum_tensor("first_all", [P, 2, 512], fp32))
                stored, loaded, sj_loaded, firsts, spread, rooted, steps, staged, out0, out1, passed = s.enter_context(semaphores(
                    nc, "stored", "loaded", "sj_loaded", "firsts", "spread", "rooted", "steps", "staged", "out0", "out1", "passed"))
                moved = (out0, out1)
                block = s.enter_context(nc.Block())
                half = J // 2

                @block.sync
                def _(sp):
                    sp.dma_start(one_partition(k["sj_edge"]), sje).then_inc(stored, 16)
                    sp.wait_ge(stored, 16)
                    for n, (to, of, sem) in enumerate(((es, k["edges"], loaded), (sj, k["sj_edge"], sj_loaded))):
                        with sp.Fori(0, PIECES) as i:
                            sp.wait_ge(staged, i * 4 + (n * 4 * PIECES + 4))
                            a = bass.ds(i * (J // PIECES), J // PIECES)
                            sp.dma_start(to[:, a, :], of.rearrange("(j p) f -> p j f", p=P)[:, a, :]).then_inc(sem, 16)
                    sp.wait_ge(sj_loaded, 16 * PIECES)

                @block.vector
                def _(dve):
                    v, ch = nc.vector, Count(steps)
                    ch.link(dve, v.tensor_scalar(root[:], k["count"][:, 0, :], 1.0, None, ALU.max))
                    ch.link(dve, v.tensor_scalar(k["alone"][:], root[:], 1.0, None, ALU.is_equal))
                    dve.wait_ge(rooted, 1)
                    v.reciprocal(k["dinv"][:], root[:])
                    with dve.Fori(0, NT) as t:
                        x = k["X"][:, bass.ds(t, 1), :]
                        v.scalar_tensor_tensor(x, XL[:, bass.ds(t, 1), :], k["alone"][:, bass.ds(t, 1)], x, ALU.mult, ALU.add)
                    dve.wait_ge(loaded, 16 * PIECES)
                    v.tensor_copy(k["d0i"][:], es[0:1, :, 1])
                    v.tensor_copy(d0[:], es[0:1, :, 1]).then_inc(firsts, 1)
                    v.tensor_copy(k["idx"][:], es[:, :, 0])
                    v.tensor_scalar(k["cap"][:], es[:, :, 2], 2.0, -BIG, ALU.is_equal, ALU.mult)
                    v.scalar_tensor_tensor(k["idx_typed"][:], es[:, :, 2], float(NP), es[:, :, 0], ALU.mult, ALU.add)
                    dve.wait_ge(spread, 1)
                    for n in range(2):
                        a = slice(n * half, (n + 1) * half)
                        v.tensor_tensor(k["dloc"][:, a], es[:, a, 1], first[:, n, 0:half], ALU.subtract)

                @block.tensor
                def _(pe):
                    pe.wait_ge(firsts, 1)
                    for n in range(2):
                        last = nc.tensor.matmul(first[:, n, 0:half], k["ones"][0:1, :], d0[0:1, n * half:(n + 1) * half],
                                                start=True, stop=True)
                    last.then_inc(spread, 1)

                @block.scalar
                def _(act):
                    act.wait_ge(steps, 2)
                    nc.scalar.activation(root[:], root[:], ACT.Sqrt).then_inc(rooted, 1)
                    with act.Fori(0, STEPS) as i:
                        for g in range(2):
                            act.wait_ge(moved[g], i * (16 * U) + 16)
                            a = bass.ds(i * G2 + g * U, U)
                            nc.scalar.activation(slot[:, g], ed[:, a, 3], ACT.Copy).then_inc(staged, 1)
                            nc.scalar.activation(row[:, g, :, 0:NH + 1], pay[:, a, :], ACT.Copy).then_inc(staged, 1)

                @block.gpsimd
                def _(pool):
                    for g in range(2):
                        pool.dma_start(k["credit"][g:g + 1, :], k["gate"][:, 0:2]).then_inc(moved[g], 16)
                    with pool.Fori(0, STEPS) as i:
                        for g in range(2):
                            pool.wait_ge(staged, i * 4 + (2 * g + 2))
                            pool.sem_inc(passed, 1)
                            for u in range(U):
                                nc.gpsimd.indirect_dma_start(
                                    k["by_src"], bass.IndirectOffsetOnAxis(ap=slot[:, g, u:u + 1], axis=0),
                                    row[:, g, u, :], None).then_inc(moved[g], 16)
                    for g in range(2):
                        pool.wait_ge(moved[g], STEPS * 16 * U + 16)

        with ExitStack() as d:
            by = d.enter_context(nc.sbuf_tensor("at_by", [P, J, 2 * NH], fp32))
            fill = d.enter_context(nc.sbuf_tensor("at_fill", [P, J, 2 * NH], fp32))
            before = d.enter_context(nc.sbuf_tensor("at_before", [P, 1], fp32))
            same = d.enter_context(nc.sbuf_tensor("at_same", [P, J], bf16))
            closed = d.enter_context(nc.sbuf_tensor("at_closed", [P, 2, NH], fp32))
            turned = d.enter_context(nc.sbuf_tensor("at_turned", [NH, 2, P], fp32))
            carry = d.enter_context(nc.sbuf_tensor("at_carry", [NH, P + 1], fp32))
            init = d.enter_context(nc.sbuf_tensor("at_init", [P, NH], fp32))
            psum = d.enter_context(nc.psum_tensor("at_ps", [P, 3, P], fp32))
            scan = acc[:, 0:J * NH].rearrange("p (j h) -> p j h", h=NH)
            val = H[:].rearrange("p t d -> p (t d)")[:, 0:J * NH].rearrange("p (j h) -> p j h", h=NH)

            def scan_over_partitions(data, gates, op0, op1, none):
                with ExitStack() as s:
                    steps, ended, flipped, carried, back = s.enter_context(semaphores(nc, "steps", "ended", "flipped", "carried", "back"))
                    block = s.enter_context(nc.Block())

                    @block.tensor
                    def _(pe):
                        pe.wait_ge(ended, 1)
                        for n in range(2):
                            last = nc.tensor.transpose(psum[0:NH, n, :], closed[:, n, :], k["ident"][:])
                        last.then_inc(flipped, 1)
                        pe.wait_ge(carried, 1)
                        nc.tensor.transpose(psum[:, 2, 0:NH], carry[:, 0:P], k["ident"][0:NH, 0:NH]).then_inc(back, 1)

                    @block.vector
                    def _(dve):
                        v, ch = nc.vector, Count(steps)
                        for h in range(NH):
                            ch.link(dve, v.tensor_tensor_scan(scan[:, :, h], gates, data[:, :, h], none, op0, op1))
                        v.tensor_copy(closed[:, 0, :], scan[:, J - 1, :])
                        ch.link(dve, v.tensor_reduce(before[:], gates, AX.X, ALU.min))
                        v.tensor_copy(closed[:, 1, :], before[:].to_broadcast([P, NH])).then_inc(ended, 1)
                        ch.link(dve, v.memset(carry[:, 0:1], none))
                        dve.wait_ge(flipped, 1)
                        ch.link(dve, v.tensor_copy(turned[:], psum[0:NH, 0:2, :]))
                        v.tensor_tensor_scan(carry[:, 1:P + 1], turned[:, 1, :], turned[:, 0, :], none, op0, op1).then_inc(carried, 1)
                        dve.wait_ge(back, 1)
                        ch.link(dve, v.tensor_copy(init[:], psum[:, 2, 0:NH]))
                        for h in range(NH):
                            ch.link(dve, v.tensor_tensor_scan(scan[:, :, h], gates, data[:, :, h], init[:, h:h + 1], op0, op1))

            with ExitStack() as s:
                loaded, reset, steps = s.enter_context(semaphores(nc, "loaded", "reset", "steps"))
                block = s.enter_context(nc.Block())

                @block.sync
                def _(sp):
                    sp.dma_start(by[:], one_partition(k["by_src"])).then_inc(loaded, 16)
                    sp.wait_ge(reset, 1)
                    sp.dma_start(before[1:P, :], one_partition(k["by_src"])[0:P - 1, J - 1, NH:NH + 1],
                                 allow_slow_non_contiguous=True).then_inc(loaded, 16)

                @block.vector
                def _(dve):
                    v, ch = nc.vector, Count(steps)
                    v.memset(before[:], -1.0).then_inc(reset, 1)
                    dve.wait_ge(loaded, 32)
                    v.tensor_copy(head_key[:], by[:, 0, NH:NH + 1])
                    v.tensor_tensor(same[:, 0:1], by[:, 0, NH:NH + 1], before[:], ALU.is_equal)
                    ch.link(dve, v.tensor_tensor(same[:, 1:J], by[:, 1:J, NH], by[:, 0:J - 1, NH], ALU.is_equal))
                    ch.link(dve, v.tensor_scalar(gate[:], same[:], -1.0, BIG, ALU.add, ALU.mult))

            scan_over_partitions(by[:, :, 0:NH], gate[:], ALU.add, ALU.max, -BIG)
            store(nc, (one_partition(k["max_scan"]), scan))
            indexed([(gathered[:, t, :], None, k["max_scan"], end[:, t:t + 1]) for t in range(NT)])
            on_vector(nc,
                      lambda v: v.tensor_tensor(gathered[:], gathered[:], score[:, :, 0:NH], ALU.add),
                      lambda v: v.scalar_tensor_tensor(row8[:, :, NH:2 * NH], gathered[:], 0.2, gathered[:], ALU.mult, ALU.max),
                      lambda v: v.tensor_copy(row8[:, :, 0:NH], score[:, :, 0:NH]))
            store(nc, (rows(k["row_node"]), row8[:]))
            indexed([(k["row_start"], start[:, 1, t:t + 1], row8[:, t, :], None) for t in range(NT)]
                    + [(head[:], None, k["row_node"], head_key[:])])
            with ExitStack() as s:
                loaded, scored, exped, steps = s.enter_context(semaphores(nc, "loaded", "scored", "exped", "steps"))
                block = s.enter_context(nc.Block())

                @block.sync
                def _(sp):
                    sp.dma_start(fill[:], one_partition(k["row_start"][0:EP, :])).then_inc(loaded, 16)

                @block.vector
                def _(dve):
                    v, ch = nc.vector, Count(steps)
                    ch.link(dve, v.tensor_copy(gate[:], same[:]))
                    ch.link(dve, v.memset(gate[:, 0:1], 0.0))
                    dve.wait_ge(loaded, 16)
                    ch.link(dve, v.tensor_copy(fill[:, 0, :], head[:]))
                    for f in range(2 * NH):
                        ch.link(dve, v.tensor_tensor_scan(fill[:, :, f], gate[:], fill[:, :, f], 0.0, ALU.mult, ALU.add))
                    ch.link(dve, v.tensor_tensor(val, fill[:, :, 0:NH], by[:, :, 0:NH], ALU.add))
                    ch.link(dve, v.scalar_tensor_tensor(val, val, 0.2, val, ALU.mult, ALU.max))
                    v.tensor_tensor(val, val, fill[:, :, NH:2 * NH], ALU.subtract).then_inc(scored, 1)

                @block.scalar
                def _(act):
                    act.wait_ge(scored, 1)
                    nc.scalar.activation(val, val, ACT.Exp).then_inc(exped, 1)

            scan_over_partitions(val, same[:], ALU.mult, ALU.add, 0.0)
            store(nc, (one_partition(k["sum_scan"]), scan))
            indexed([(gathered[:, t, :], None, k["sum_scan"], end[:, t:t + 1]) for t in range(NT)])

        with ExitStack() as d:
            tab = d.enter_context(nc.sbuf_tensor("at_tab", [P, NT, AW], fp32))
            on_vector(nc,
                      lambda v: v.tensor_scalar(gathered[:], gathered[:], 1e-16, None, ALU.add),
                      lambda v: v.reciprocal(gathered[:], gathered[:]),
                      *[lambda v, h=h: v.tensor_tensor(tab[:, :, h * HC:(h + 1) * HC], XL[:, :, h * HC:(h + 1) * HC],
                                                  gathered[:, :, h:h + 1].to_broadcast([P, NT, HC]), ALU.mult) for h in range(NH)],
                      lambda v: v.tensor_copy(tab[:, :, D:AW], row8[:]))
            store(nc, (rows(k["table0"]), tab[:]))


def layers(nc, k):
    X, H, w, ball, dinv = (k[n] for n in ("X", "H", "w", "ball", "dinv"))
    wide = lambda tiles, n=D: dinv[:, tiles].unsqueeze(2).to_broadcast([P, NG, n])
    bias = lambda b, n=D: b.unsqueeze(1).to_broadcast([P, NG, n])

    def into(dest, b, width=D):
        return lambda v, t, got: v.tensor_tensor(dest[:, t, :], got, bias(b, width), ALU.add)

    def convolved(b):
        return [lambda v, t, got: v.tensor_tensor(H[:, t, :], got, wide(t), ALU.mult),
                lambda v, t, got: v.tensor_tensor(H[:, t, :], H[:, t, :], bias(b), ALU.add)]

    relu_times_dinv = lambda v, t, got: v.scalar_tensor_tensor(H[:, t, :], H[:, t, :], 0.0, wide(t), ALU.max, ALU.mult)
    add_relu = lambda v, t, got: v.scalar_tensor_tensor(X[:, t, :], H[:, t, :], 0.0, X[:, t, :], ALU.max, ALU.add)

    with nc.sbuf_tensor("sj_chunks", [P, J, NH], fp32) as sj, ExitStack() as s:
        XL = s.enter_context(nc.sbuf_tensor("XL", [P, NT, D], fp32))
        score = s.enter_context(nc.sbuf_tensor("score", [P, NT, 2 * NH], fp32))
        row8 = s.enter_context(nc.sbuf_tensor("row8", [P, NT, 2 * NH], fp32))
        node_stage(nc, k, "xl", norm=True, products=[
            (w["0"][:], D, into(XL, ball[:, 3, :])), (w["att"][:], 2 * NH, into(score, k["batt_all"][:], 2 * NH))])
        attention_rows(nc, k | {"XL": XL}, score, row8, sj)
        s.close()
        aggregate(nc, k, "ag0", k["table0"], k["idx"], AW, D, attend=(sj, k["cap"]))

    with ExitStack() as s:
        made = [s.enter_context(nc.sbuf_tensor(f"made1{n}", [P, NT, D], fp32)) for n in range(3)]
        kind = lambda n: rows(k["table1"][n * NP:(n + 1) * NP, :])
        node_stage(nc, k, "layer1", feat=D, norm=True,
                   land=[lambda v, t, got: v.tensor_tensor(X[:, t, :], X[:, t, :], got, ALU.add)],
                   products=[(w["1"][:, n, :], D, into(made[n], ball[:, 4 + n, :])) for n in range(3)],
                   store=lambda sp, t, last: [sp.dma_start(kind(n)[:, t, :], made[n][:, t, :]) for n in range(3)])
    aggregate(nc, k, "ag1", k["table1"], k["idx_typed"], D, D)

    node_stage(nc, k, "layer2", feat=D, norm=True,
               land=[lambda v, t, got: v.scalar_tensor_tensor(X[:, t, :], got, 0.0, X[:, t, :], ALU.max, ALU.add)],
               after=lambda v, t: v.tensor_tensor(H[:, t, :], H[:, t, :], wide(t), ALU.mult),
               store=lambda sp, t, last: [sp.dma_start(rows(k["table2"][0])[:, t, :], H[:, t, :])])
    aggregate(nc, k, "ag2a", k["table2"][0], k["idx"], D, D)
    node_stage(nc, k, "mid2", feat=D, weight=w["21"][:],
               land=convolved(ball[:, 0, :]) + [relu_times_dinv],
               store=lambda sp, t, last: [sp.dma_start(rows(k["table2"][1])[:, t, :], H[:, t, :])])
    aggregate(nc, k, "ag2b", k["table2"][1], k["idx"], D, D)

    with ExitStack() as s:
        narrow = s.enter_context(nc.sbuf_tensor("narrow", [P, NT, D3], fp32))
        scaled = lambda v, t, got: v.tensor_tensor(narrow[:, t, :], got, wide(t, D3), ALU.mult)
        save = lambda n: lambda sp, t, last: [sp.dma_start(rows(k["table3"][n])[:, t, :], narrow[:, t, :])]
        node_stage(nc, k, "layer3", feat=D, weight=w["22"][:], norm=True, land=convolved(ball[:, 1, :]) + [add_relu],
                   products=[(w["31"][:], D3, scaled)], store=save(0))
        aggregate(nc, k, "ag3a", k["table3"][0], k["idx"], D3, D3)
        node_stage(nc, k, "mid3", feat=D3, store=save(1), land=[
            scaled,
            lambda v, t, got: v.tensor_tensor(narrow[:, t, :], narrow[:, t, :], bias(k["b31_all"][:], D3), ALU.add),
            lambda v, t, got: v.tensor_tensor(narrow[:, t, :], narrow[:, t, :], wide(t, D3), ALU.mult)])
        aggregate(nc, k, "ag3b", k["table3"][1], k["idx"], D3, D3)

    full = N // P

    def save_out(sp, t, last):
        whole = k["out"][0:full * P, :].rearrange("(t p) d -> p t d", p=P)
        if not last:
            return [sp.dma_start(whole[:, t, :], X[:, t, :])]
        return [sp.dma_start(whole[:, t.start:full, :], X[:, t.start:full, :]),
                sp.dma_start(k["out"][full * P:N, :], X[0:N - full * P, full, :])]

    node_stage(nc, k, "last", feat=D3, weight=w["32"][:], land=convolved(ball[:, 2, :]) + [add_relu], store=save_out)


_WEIGHTS = ["L0_gnn_W_lin", "L0_gnn_b_lin", "L0_gnn_W_att", "L0_gnn_b_att", "L1_gnn_W_data", "L1_gnn_b_data",
            "L1_gnn_W_control", "L1_gnn_b_control", "L1_gnn_W_self", "L1_gnn_b_self", "L2_gnn_W1", "L2_gnn_b1",
            "L2_gnn_W2", "L2_gnn_b2", "L3_gnn_W1", "L3_gnn_b1", "L3_gnn_W2", "L3_gnn_b2"]


def kernel(**inputs):
    import numpy as _np
    import concourse.bacc as _bacc
    from concourse import mybir as _mybir
    from concourse.bass_utils import run_bass_kernel_spmd as _run

    nodes = _np.arange(N, dtype=_np.int32)
    pads = _np.full(EP - E - N, N, _np.int32)

    def columns(*parts):
        return _np.ascontiguousarray(_np.concatenate([_np.asarray(a) for a in parts]).reshape(J, P).T)

    arrays = {
        "x": _np.concatenate([_np.asarray(inputs["x"]), _np.zeros((NP - N, D), _np.float32)]),
        "e_src": columns(inputs["src"], nodes, pads),
        "e_dst": columns(inputs["dst"], nodes, pads),
        "e_type": columns(inputs["edge_type_2"], _np.full(EP - E, 2, _np.int32)),
    }
    for name in _WEIGHTS:
        a = _np.ascontiguousarray(inputs[name])
        arrays[name] = a if a.ndim == 2 else a.reshape(1, -1)
    nc = _bacc.Bacc("TRN2", target_bir_lowering=False, num_devices=1)
    args = [nc.dram_tensor(n, a.shape, _mybir.dt.from_np(a.dtype), kind="ExternalInput").ap() for n, a in arrays.items()]
    out = nc.dram_tensor("out", (N, D), _mybir.dt.float32, kind="ExternalOutput").ap()
    gnn_kernel(nc, *args, out)
    r = _run(nc, [arrays], core_ids=[0])
    return r.results[0]["out"]
```
